# Optimizing a Trainium2 kernel written in Bass

```python
import numpy as np
import jax
import jax.numpy as jnp

def _softmax(x, axis=-1):
    return jax.nn.softmax(x, axis=axis)

def _gelu(x):
    return jax.nn.gelu(x, approximate=True)

def _silu(x):
    return jax.nn.silu(x)

def _sigmoid(x):
    return jax.nn.sigmoid(x)

def _layernorm(x, axis=-1, eps=1e-05):
    m = jnp.mean(x, axis=axis, keepdims=True)
    v = jnp.var(x, axis=axis, keepdims=True)
    return (x - m) / jnp.sqrt(v + eps)

def _scatter_add(tgt, idx, src, axis=0):
    return tgt.at[idx].add(src)

def _segment_sum(src, seg, n):
    return jax.ops.segment_sum(src, seg, n)
kernel_name = 'mk_adaln_d1_jaxref_r4_df1b01'

def setup_inputs(seed: int=0):
    np.random.seed(seed)
    _w = jnp.asarray

    def _L0_attn_setup():
        import jax, jax.numpy as jnp
        import numpy as np
        B, T, C, H = (2, 512, 512, 16)
        HD = C // H
        BASE = 10000.0

        def _rope_tables(seq_len, d):
            p = jnp.arange(d // 2, dtype=jnp.float32)
            theta = jnp.power(BASE, -2.0 ** p / d)
            pos = jnp.arange(1, seq_len + 1, dtype=jnp.float32)[:, None]
            c = pos * theta
            ang = jnp.concatenate([c, c], axis=-1)
            return (jnp.cos(ang), jnp.sin(ang))

        def _rope(x):
            d = x.shape[-1]
            cos, sin = _rope_tables(x.shape[-2], d)
            half = d // 2
            x_rot = jnp.concatenate([-x[..., half:], x[..., :half]], axis=-1)
            return x * cos + x_rot * sin
        key = jax.random.key(seed)
        k1, k2, k3 = jax.random.split(key, 3)
        x = jax.random.normal(k1, (B, T, C), dtype=jnp.float32)
        Wqkv = jax.random.normal(k2, (3 * C, C), dtype=jnp.float32) * 0.02
        bqkv = jnp.zeros((3 * C,), dtype=jnp.float32)
        Wo = jax.random.normal(k3, (C, C), dtype=jnp.float32) * 0.02
        bo = jnp.zeros((C,), dtype=jnp.float32)
        return {'x': x, 'Wqkv': Wqkv, 'bqkv': bqkv, 'Wo': Wo, 'bo': bo}
    _L0_attn_in = _L0_attn_setup()

    def _L0_ffn_setup():
        import jax, jax.numpy as jnp
        import numpy as np
        NUM_EXPERTS = 128
        NUM_KEPT = 48
        TOP_K = 8
        HIDDEN = 512
        INTER = 192
        CAP = 192
        BATCH, SEQ = (2, 256)
        key = jax.random.key(seed)
        k1, k2, k3, k4 = jax.random.split(key, 4)
        hidden_states = jax.random.normal(k1, (BATCH, SEQ, HIDDEN), jnp.float32)
        gate_weight = jax.random.normal(k2, (NUM_EXPERTS, HIDDEN), jnp.float32) * 0.02
        gate_up_proj = jax.random.normal(k3, (NUM_KEPT, 2 * INTER, HIDDEN), jnp.float32) * 0.02
        down_proj = jax.random.normal(k4, (NUM_KEPT, HIDDEN, INTER), jnp.float32) * 0.02
        o2n = -np.ones(NUM_EXPERTS, np.int32)
        o2n[np.arange(NUM_KEPT) * 2] = np.arange(NUM_KEPT, dtype=np.int32)
        old_to_new = jnp.asarray(o2n)
        return {'hidden_states': hidden_states, 'gate_weight': gate_weight, 'gate_up_proj': gate_up_proj, 'down_proj': down_proj, 'old_to_new': old_to_new}
    _L0_ffn_in = _L0_ffn_setup()
    _L0_c = _w((lambda *s: np.random.randn(*s).astype(np.float32) * 0.05)(4, 512))
    _L0_wmod = _w((lambda *s: np.random.randn(*s).astype(np.float32) * 0.05)(512, 6 * 512) * 512 ** (-0.5))
    _d = {'L0_attn_x': _L0_attn_in['x'], 'L0_attn_Wqkv': _L0_attn_in['Wqkv'], 'L0_attn_bqkv': _L0_attn_in['bqkv'], 'L0_attn_Wo': _L0_attn_in['Wo'], 'L0_attn_bo': _L0_attn_in['bo'], 'L0_ffn_gate_weight': _L0_ffn_in['gate_weight'], 'L0_ffn_gate_up_proj': _L0_ffn_in['gate_up_proj'], 'L0_ffn_down_proj': _L0_ffn_in['down_proj'], 'L0_ffn_old_to_new': _L0_ffn_in['old_to_new'], 'L0_c': _L0_c, 'L0_wmod': _L0_wmod}
    _x0 = _d['L0_attn_x']
    _d['L0_attn_x'] = jax.random.normal(jax.random.fold_in(jax.random.key(seed), 1), (4, 2048, 512), dtype=_x0.dtype)
    del _x0
    return _d

def reference(L0_attn_x, L0_attn_Wqkv, L0_attn_bqkv, L0_attn_Wo, L0_attn_bo, L0_ffn_gate_weight, L0_ffn_gate_up_proj, L0_ffn_down_proj, L0_ffn_old_to_new, L0_c, L0_wmod):

    def _L0_attn_ref(x, Wqkv, bqkv, Wo, bo):
        import jax, jax.numpy as jnp
        import numpy as np
        B, T, C, H = (2, 512, 512, 16)
        HD = C // H
        BASE = 10000.0

        def _rope_tables(seq_len, d):
            p = jnp.arange(d // 2, dtype=jnp.float32)
            theta = jnp.power(BASE, -2.0 ** p / d)
            pos = jnp.arange(1, seq_len + 1, dtype=jnp.float32)[:, None]
            c = pos * theta
            ang = jnp.concatenate([c, c], axis=-1)
            return (jnp.cos(ang), jnp.sin(ang))

        def _rope(x):
            d = x.shape[-1]
            cos, sin = _rope_tables(x.shape[-2], d)
            half = d // 2
            x_rot = jnp.concatenate([-x[..., half:], x[..., :half]], axis=-1)
            return x * cos + x_rot * sin
        b, t, c = x.shape
        qkv = x @ Wqkv.T + bqkv
        q, k, v = jnp.split(qkv, 3, axis=-1)

        def to_heads(z):
            return z.reshape(b, t, H, HD).transpose(0, 2, 1, 3)
        q, k, v = (to_heads(q), to_heads(k), to_heads(v))
        q = _rope(q)
        k = _rope(k)
        scale = 1.0 / jnp.sqrt(jnp.float32(HD))
        att = jnp.einsum('bhqd,bhkd->bhqk', q, k) * scale
        causal = jnp.tril(jnp.ones((t, t), dtype=bool))
        att = jnp.where(causal, att, -jnp.inf)
        att = jax.nn.softmax(att, axis=-1)
        y = jnp.einsum('bhqk,bhkd->bhqd', att, v)
        y = y.transpose(0, 2, 1, 3).reshape(b, t, c)
        y = y @ Wo.T + bo
        return y

    def _L0_ffn_ref(hidden_states, gate_weight, gate_up_proj, down_proj, old_to_new):
        import jax, jax.numpy as jnp
        import numpy as np
        NUM_EXPERTS = 128
        NUM_KEPT = 48
        TOP_K = 8
        HIDDEN = 512
        INTER = 192
        CAP = 192
        BATCH, SEQ = (2, 256)
        B, S, H = hidden_states.shape
        x = hidden_states.reshape(-1, H)
        T = x.shape[0]
        logits = x @ gate_weight.T
        logits = jnp.where(old_to_new[None, :] == -1, -jnp.inf, logits)
        probs = jax.nn.softmax(logits.astype(jnp.float32), axis=-1).astype(logits.dtype)
        top_v, top_i = jax.lax.top_k(probs, TOP_K)
        top_v = top_v / jnp.sum(top_v, axis=-1, keepdims=True)
        sel_new = old_to_new[top_i]
        E = gate_up_proj.shape[0]
        flat_e = sel_new.reshape(-1)
        flat_w = top_v.reshape(-1)
        tok = jnp.repeat(jnp.arange(T), TOP_K)
        oh = (flat_e[:, None] == jnp.arange(E)[None, :]).astype(jnp.int32)
        pos = jnp.sum(jnp.cumsum(oh, axis=0) * oh, axis=-1) - 1
        valid = pos < CAP
        pos_c = jnp.where(valid, pos, CAP)
        xb = jnp.zeros((E, CAP + 1, H), x.dtype).at[flat_e, pos_c].set(x[tok])
        xb = xb[:, :CAP]
        gu = jnp.einsum('ech,eoh->eco', xb, gate_up_proj)
        g, u = jnp.split(gu, 2, axis=-1)
        h = jax.nn.silu(g) * u
        out = jnp.einsum('eci,ehi->ech', h, down_proj)
        y = out[flat_e, jnp.minimum(pos_c, CAP - 1)]
        w = flat_w * valid.astype(flat_w.dtype)
        final = jnp.zeros_like(x).at[tok].add(y * w[:, None])
        return final.reshape(B, S, H)
    x = L0_attn_x
    mod = (_silu(L0_c) @ L0_wmod).reshape(L0_c.shape[0], 6, 1, -1)
    sa, ca, ga, sb, cb, gb = (mod[:, 0], mod[:, 1], mod[:, 2], mod[:, 3], mod[:, 4], mod[:, 5])
    ga = (2 * (ga >= 0) - 1) * jnp.maximum(jnp.abs(ga), 0.25)
    gb = (2 * (gb >= 0) - 1) * jnp.maximum(jnp.abs(gb), 0.25)
    h = _layernorm(x, axis=-1) * (1 + ca) + sa
    x = x + ga * _L0_attn_ref(h, L0_attn_Wqkv, L0_attn_bqkv, L0_attn_Wo, L0_attn_bo)
    h = _layernorm(x, axis=-1) * (1 + cb) + sb
    x = x + gb * _L0_ffn_ref(h, L0_ffn_gate_weight, L0_ffn_gate_up_proj, L0_ffn_down_proj, L0_ffn_old_to_new)
    return x

_drawn_inputs = setup_inputs


def setup_inputs(seed=0):
    import zlib

    import numpy as np

    out = dict(_drawn_inputs(seed))
    spreads = {'L0_attn_bqkv': (0.0, 0.669), 'L0_attn_bo': (0.0, 0.331)}
    factors = {'L0_attn_Wqkv': 8.0,
     'L0_attn_Wo': 4.521,
     'L0_ffn_gate_weight': 8.0,
     'L0_ffn_gate_up_proj': 8.0,
     'L0_ffn_down_proj': 8.0}
    for name, (base, spread) in spreads.items():
        noise = np.random.default_rng([zlib.crc32(name.encode()), seed]).standard_normal(out[name].shape)
        drawn = base * np.exp(spread * noise) if base else spread * noise
        out[name] = jnp.asarray(drawn.astype(out[name].dtype))
    for name, factor in factors.items():
        out[name] = (out[name] * factor).astype(out[name].dtype)
    return out
```

```python
from contextlib import ExitStack

import numpy as np

import concourse.bass as bass
from concourse import mybir

F32 = mybir.dt.float32
F32R = mybir.dt.float32r
BF16 = mybir.dt.bfloat16
I32 = mybir.dt.int32
ALU = mybir.AluOpType
ACT = mybir.ActivationFunctionType
AX = mybir.AxisListType

P = 128
NB, T, C, H, HD = 4, 2048, 512, 16, 32
KT = C // P
CH = 512
NCH = T // CH
TPC = CH // P
NT = T // P
GH = P // HD
NG = H // GH
NTOK = NB * T
NOLD, NEW, TOPK = 128, 48, 8
CAP, INTER = 192, 192
HALF = CAP // 2
ROW = C + NEW
NROW = NTOK + HALF
EPS = 1e-5
SCALE = float(HD) ** -0.5
NEG = -1e30
FLOOR = -104.0
BIG = 16384.0
SA, CA1, GA, SB, CB1, GB = range(6)

K_ID, K_NEG, K_U, K_ONE = 0, 128, 640, 768
K_I48, K_A16, K_B16, K_P1, K_BD, K_DUM, K_T4 = 896, 944, 960, 976, 977, 985, 1001
K_MH = 1005
K_MT = 1009
NK = 1265


ONE = 1


def constants():
    k = np.zeros((P, NK), np.float32)
    p = np.arange(P)
    k[:, K_ID:K_ID + P] = np.eye(P)
    k[:, K_NEG + 384:K_NEG + 512] = np.where(p[None, :] > p[:, None], NEG, 0.0)
    k[:, K_U:K_U + P] = p[:, None] < p[None, :]
    k[:, K_ONE:K_ONE + P] = 1.0
    k[:, K_I48:K_I48 + NEW] = np.arange(NEW)
    k[:, K_A16:K_A16 + 16] = 16.0 * np.arange(16)
    k[:, K_B16:K_B16 + 16] = np.arange(16)
    k[:, K_P1] = p + 1
    k[:, K_BD:K_BD + 8] = p[:, None] // 16 == np.arange(8)[None, :]
    k[:, K_DUM:K_DUM + 16] = NTOK + 1 + (16 * (p[:, None] % 16) + np.arange(16)[None, :]) % HALF
    k[:, K_T4:K_T4 + TPC] = np.arange(TPC)
    k[:, K_MT:K_MT + P] = NEG
    k[:, K_MT + P:K_MT + 2 * P] = np.where(p[:, None] > p[None, :], NEG, 0.0)
    k[:, K_MH:K_MH + TPC] = -0.5
    return k


def rope_tables():
    d = np.arange(HD // 2, dtype=np.float32)
    theta = np.power(np.float32(10000.0), (-np.power(np.float32(2.0), d) / np.float32(HD)).astype(np.float32)).astype(np.float32)
    pos = np.arange(1, T + 1, dtype=np.float32)
    ang = (theta[:, None] * pos[None, :]).astype(np.float32)
    cos = np.cos(ang).astype(np.float32)
    sin = np.sin(ang).astype(np.float32)
    return (np.tile(np.concatenate([cos, cos]), (GH, 1)),
            np.tile(np.concatenate([-sin, sin]), (GH, 1)))


def plan():
    tiles = [(qb, c, min(CH, (qb + 1) * P - c * CH)) for qb in range(NT) for c in range(qb // TPC + 1)]
    units = []
    for j in range(NCH):
        units += [(j, kb, 0, False) for kb in range(0, TPC * j, 2)]
        units += [(j, TPC * j, 0, True), (j, TPC * j + 2, 2 * P, True)]
    return tiles, units


TILES, UNITS = plan()
NTILE, NU = len(TILES), len(UNITS)
NS1 = GH * (NTILE + 1)
NS2 = GH * NU
PER_UNIT = 3


def schedule():
    out = [("max", 0, i) for i in range(NTILE)] + [("row", 0)]
    late = []
    for h in range(GH):
        left = [("max", h + 1, i) for i in range(NTILE)] + [("row", h + 1)] if h + 1 < GH else []
        for u in range(NU):
            out.append(("score", h, u))
            out += left[:PER_UNIT]
            left = left[PER_UNIT:]
            out += late
            late = []
            if u:
                out.append(("value", h, u - 1))
                if UNITS[u][0] != UNITS[u - 1][0]:
                    late.append(("norm", h, UNITS[u - 1][0]))
            elif h:
                out.append(("value", h - 1, NU - 1))
                late.append(("norm", h - 1, NCH - 1))
        assert not left
    return out + late + [("value", GH - 1, NU - 1), ("norm", GH - 1, NCH - 1)]


class Chain:

    def __init__(self, eng, sem, per):
        self.eng, self.sem, self.per = eng, sem, per

    def begin(self, n):
        self.base, self.k = n * self.per, 0

    def link(self, ins, passed=None):
        ins.then_inc(self.sem, 1)
        self.k += 1
        self.eng.wait_ge(self.sem, ONE + self.base + self.k)
        if passed is not None:
            self.eng.sem_inc(passed, 1)

    def end(self):
        assert self.k == self.per, self.k


def adaln_block(nc, x, wqkv, bqk, bv, wo, bo, cT, wmod, gwT, o2n_col, o2n_row, wgu, wdn, cos, sin, kst, out):
    with ExitStack() as ctx:
        sems = []

        def sem(name, bumped=True):
            s = ctx.enter_context(nc.semaphore(name))
            if bumped:
                sems.append(s)
            return s

        def dram(name, shape, dt=F32):
            return nc.dram_tensor(name, shape, dt, kind="Internal").ap()

        modd = dram("modd", [NB, 6 * C])
        gbd = dram("gbd", [NB + 1, C])
        otd = dram("otd", [NB, NG, P, T])
        table = dram("table", [NROW, ROW])
        idxd = dram("idxd", [2, NEW * 256], I32)

        at = [0]

        def place(name, shape, dt):
            size = int(np.prod(shape[1:])) * (2 if dt == BF16 else 4)
            t = nc.alloc_sbuf_tensor_at(name, shape, dt, offset=BASE + at[0])
            at[0] += (size + 63) // 64 * 64
            return t

        BASE = (nc.sbuf_base + 63) // 64 * 64

        K = place("consts", [P, NK], F32)
        hT = place("hT", [P, KT, T], F32)
        modc = place("modc", [P, NB, 2 * KT], F32)
        Ubf = place("Ubf", [P, P], BF16)
        onesbf = place("onesbf", [P, P], BF16)
        idbf = place("idbf", [P, P], BF16)
        mtbf = place("mtbf", [P, 2 * P], BF16)
        Mold = place("Mold", [P, NEW], F32)
        Mbf = place("Mbf", [P, NEW], BF16)
        negb = place("negb", [P, NOLD], F32)
        Racc = place("Racc", [P, 6, 256], F32)
        tot = place("tot", [P, NEW], F32)
        tcol = place("tcol", [P, TPC], F32)
        gwt = place("gwt", [P, KT, NOLD], F32)
        PHASE = at[0]

        csT = place("csT", [P, KT, NB], F32)
        ce = place("ce", [P, KT, NB], F32)
        wm = place("wm", [P, KT, 6 * C], F32)
        mods = place("mods", [NB, 6 * C], F32)
        sgn = place("sgn", [NB, C], F32)
        oc = place("oc", [P, 1], I32)
        ocf = place("ocf", [P, 1], F32)
        orow = place("orow", [P, NOLD], I32)
        zrow = place("zrow", [HALF, ROW], F32)

        at[0] = PHASE
        cs = place("cs", [P, 2, T], F32)
        W = place("W", [P, KT, 3 * P], F32)
        bqg = place("bqg", [P, 2], F32)
        bvg = place("bvg", [P, P], F32)
        part = place("part", [P, NT, NCH], F32)
        mx = place("mx", [P, NT], F32)
        mT = place("mT", [NT, P], F32R)
        QK = place("QK", [P, GH, 2, T], F32R)
        st = place("st", [P, 2, 4, CH], F32R)
        V = place("V", [P, NT, GH, 2 * HD], F32)
        den = place("den", [P, T], F32)
        ot = place("ot", [P, T], F32)
        at_pr = at[0]
        Pr = place("Pr", [P, 4, 2, CH], F32)
        at[0] = at_pr
        qraw = place("qraw", [P, 2, CH], F32)
        qs = place("qs", [P, 2, CH], F32)
        t1 = place("t1", [P, 2, CH], F32)

        at[0] = PHASE
        xin = place("xin", [P, 2, TPC, C], F32)
        xhat = place("xhat", [P, TPC, C], F32)
        stA = place("stA", [P, TPC, 6], F32)
        mvA = place("mvA", [P, TPC, 2], F32)
        rsA = place("rsA", [P, TPC], F32)

        at[0] = PHASE
        wot = place("wot", [P, KT, C], F32)
        rows = place("rows", [P, 5, C], F32)
        otc = place("otc", [P, KT, CH], F32)
        xc = place("xc", [P, TPC, C], F32)
        x1 = place("x1", [P, TPC, C], F32)
        h2 = place("h2", [P, TPC, C], F32)
        h2T = place("h2T", [P, KT, CH], F32)
        stC = place("stC", [P, TPC, 6], F32)
        mvC = place("mvC", [P, TPC, 2], F32)
        rsC = place("rsC", [P, TPC], F32)
        key = place("key", [P, TPC, NOLD], F32)
        lmx = place("lmx", [P, TPC], F32)
        ex = place("ex", [P, TPC, NOLD], F32)
        top = place("top", [P, TPC, 8], F32)
        rep = place("rep", [P, TPC, NOLD], F32)
        msk = place("msk", [P, TPC, NOLD], F32)
        gs = place("gs", [P, TPC], F32)
        gT = place("gT", [P, TPC, P], F32)
        mTb = place("mTb", [P, TPC, P], BF16)
        gN = place("gN", [P, TPC, NEW], F32)
        mN = place("mN", [P, TPC, NEW], BF16)
        pos = place("pos", [P, TPC, NEW], F32)
        posi = place("posi", [P, TPC, NEW], I32)
        hi = place("hi", [P, TPC, NEW], I32)
        lo = place("lo", [P, TPC, NEW], I32)
        Aoh = place("Aoh", [P, TPC, NEW, 16], BF16)
        B1 = place("B1", [P, TPC, 6, P], BF16)
        B2 = place("B2", [P, TPC, 6, 2, P], BF16)

        at[0] = PHASE
        Rd = place("Rd", [P, 6, 2, 8, 16], F32)
        slot = place("slot", [P, 6, 2, 16], F32)
        tok1 = place("tok1", [P, 6, 16], F32)
        emp = place("emp", [P, 6, 16], F32)
        sidx = place("sidx", [P, 2, 6, 16], I32)
        it = place("it", [HALF, 2, 2, 2], I32)
        X = place("X", [HALF, 2, 2, ROW], F32)
        GBr = place("GBr", [HALF, 2, 2, C], F32)
        Wg = place("Wg", [P, 2, KT, 2 * INTER], F32)
        Wd = place("Wd", [HALF, 2, 2, C], F32)
        XT = place("XT", [P, 2, 2, CAP], F32)
        e1 = place("e1", [HALF, 2, CAP], F32)
        hb = place("hb", [HALF, 2, CAP], F32)
        wv = place("wv", [HALF, 2, 2], F32)
        z = place("z", [HALF, 2, 2, C], F32)

        PS = ctx.enter_context(nc.psum_tensor("PS", [P, 8, 512], F32))
        S1 = [PS[:, 0], PS[:, 1]]
        S2 = [PS[:, 2:4], PS[:, 4:6]]
        O = [PS[:, 6], PS[:, 7]]

        ident = K[:, K_ID:K_ID + P]

        consts_in = sem("consts_in")
        passed = sem("passed")
        mod_in = sem("mod_in")
        prep = sem("prep")
        silu_e = sem("silu_e")
        cs_ready = sem("cs_ready")
        mod_ps = sem("mod_ps")
        mod_sb = sem("mod_sb")
        mod_done = sem("mod_done")
        modT_ps = sem("modT_ps")
        modT_sb = sem("modT_sb")
        mod_out = sem("mod_out")
        zero_ready = sem("zero_ready")
        phase = sem("phase")

        x_in = [sem("x_in0"), sem("x_in1")]
        xhat_ready = sem("xhat_ready")
        hT_ps = sem("hT_ps")
        hT_sb = sem("hT_sb")
        chA = sem("chA")
        var_ready = sem("var_ready")
        rs_done = sem("rs_done")
        varC_ready = sem("varC_ready")
        rsC_done = sem("rsC_done")

        w_in = sem("w_in")
        ones_set = sem("ones_set")
        qk_ps = sem("qk_ps")
        v_ps = sem("v_ps")
        v_sb = sem("v_sb")
        q_raw = sem("q_raw")
        q_shuf = sem("q_shuf")
        rope_mul = sem("rope_mul")
        rope_add = sem("rope_add")
        q_hi = sem("q_hi")
        q_lo = sem("q_lo")
        qk_in = [sem("qk_in0"), sem("qk_in1")]
        s1_ready = sem("s1_ready")
        s1_free = sem("s1_free")
        max_all = sem("max_all")
        mrow_in = sem("mrow_in")
        s2_ready = sem("s2_ready")
        exp_done = sem("exp_done")
        pv_done = sem("pv_done")
        o_rec = sem("o_rec")
        o_norm = sem("o_norm")
        den_inv = sem("den_inv")
        ot_ready = sem("ot_ready")
        ot_out = sem("ot_out")

        rows_in = sem("rows_in")
        c_in = sem("c_in")
        gabo = sem("gabo")
        xg_ready = sem("xg_ready")
        y_ps = sem("y_ps")
        y_used = sem("y_used")
        x1_ready = sem("x1_ready")
        h2_ready = sem("h2_ready")
        c_out = sem("c_out")
        t_ps = sem("t_ps")
        t_sb = sem("t_sb")
        l_ps = sem("l_ps")
        key_ready = sem("key_ready")
        ex_ready = sem("ex_ready")
        g_ready = sem("g_ready")
        gt_ps = sem("gt_ps")
        gt_sb = sem("gt_sb")
        n_ps = sem("n_ps")
        n_sb = sem("n_sb")
        g_out = sem("g_out")
        p_ps = sem("p_ps")
        pos_ready = sem("pos_ready")
        ab_ready = sem("ab_ready")
        r_ps = sem("r_ps")
        r_sb = sem("r_sb")
        chC = sem("chC")

        chD = sem("chD")
        slots_sb = sem("slots_sb")
        slots_out = sem("slots_out")
        it_in = [sem("it_in0"), sem("it_in1")]
        we_in = [sem("we_in0"), sem("we_in1")]
        xg_in = [sem("xg_in0", False), sem("xg_in1", False)]
        xt_ps = sem("xt_ps")
        xt_sb = sem("xt_sb")
        gu_ps = sem("gu_ps")
        e_ready = sem("e_ready")
        chE = sem("chE")
        h_ready = sem("h_ready")
        d_ps = sem("d_ps")
        wv_ready = sem("wv_ready")
        z_ready = sem("z_ready")
        scat = sem("scat", False)

        ENGINES = 5
        LOADED = 6 * 16

        def wait_apart(eng, sem, value):
            eng.wait_ge(sem, value if sem in (scat, *xg_in) else ONE + value)
            eng.sem_inc(passed, 1)

        def meet(eng, n):
            eng.sem_inc(passed, 1)
            eng.drain().then_inc(phase, 1)
            wait_apart(eng, phase, ENGINES * n)

        block = ctx.enter_context(nc.Block())

        @block.sync
        def _(sp):
            for s in sems:
                sp.sem_inc(s, ONE)
            for dst, src in ((K[:, :], kst), (csT[:, :, :], cT), (wm[:, :, :], wmod), (gwt[:, :, :], gwT),
                             (oc[:, :], o2n_col), (orow[:, :], o2n_row.partition_broadcast(P))):
                sp.dma_start(dst, src).then_inc(consts_in, 16)
            wait_apart(sp, mod_done, 1)
            wait_apart(sp, zero_ready, 1)
            sp.dma_start(modd, mods[:, :]).then_inc(mod_out, 16)
            sp.dma_start(gbd[0:NB, :], mods[:, GB * C:(GB + 1) * C]).then_inc(mod_out, 16)
            sp.dma_start(gbd[NB:NB + 1, :], zrow[0:1, 0:C]).then_inc(mod_out, 16)
            sp.dma_start(table[NTOK:NROW, :], zrow[:, :]).then_inc(mod_out, 16)
            sp.dma_start(out[NTOK:NROW, :], zrow[:, 0:C]).then_inc(mod_out, 16)
            wait_apart(sp, mod_out, 80)

            with sp.Fori(0, NB) as b:
                meet(sp, 3 * b + 1)
                with sp.Fori(0, NCH // 2) as jj:
                    for u in range(2):
                        wait_apart(sp, xhat_ready, TPC * (NCH * b + 2 * jj))
                        sp.dma_start(xin[:, u], x[b, 2 * jj + u].rearrange("(t p) c -> p t c", p=P)).then_inc(x_in[u], 16)
                meet(sp, 3 * b + 2)
                sp.dma_start(cs[:, 0], cos).then_inc(w_in, 16)
                sp.dma_start(cs[:, 1], sin).then_inc(w_in, 16)
                with sp.Fori(0, NG) as g:
                    gi = 4 * b + g
                    wait_apart(sp, v_ps, NCH * gi)
                    wait_apart(sp, v_sb, NCH * gi)
                    wait_apart(sp, q_raw, 2 * NCH * gi)
                    sp.dma_start(W[:, :, :], wqkv[g]).then_inc(w_in, 16)
                    sp.dma_start(bqg[:, :], bqk[g]).then_inc(w_in, 16)
                    sp.dma_start(bvg[:, :], bv[g].partition_broadcast(P)).then_inc(w_in, 16)
                    for j in range(NCH):
                        wait_apart(sp, q_lo, NCH * gi + j + 1)
                        wait_apart(sp, pv_done, NS2 * gi)
                        cols = slice(j * CH, (j + 1) * CH)
                        s = st[:, j % 2]
                        for h in range(GH):
                            own = slice(h * HD, (h + 1) * HD)
                            for blk, pair in enumerate((s[own, 0::2], s[own, 1:3], s[own, 0::3])):
                                sp.dma_start(QK[blk * HD:(blk + 1) * HD, h, :, cols].bitcast(F32), pair.bitcast(F32)).then_inc(qk_in[j % 2], 16)
                    for h in range(GH):
                        wait_apart(sp, s1_free, NS1 * gi + (NTILE + 1) * (h + 1))
                        sp.dma_start(QK[3 * HD:3 * HD + 1, h, 0, :].bitcast(F32), mT[:, :].bitcast(F32)).then_inc(mrow_in, 16)
                    wait_apart(sp, ot_ready, gi + 1)
                    sp.dma_start(otd[b, g], ot[:, :]).then_inc(ot_out, 16)
                wait_apart(sp, ot_out, 64 * (b + 1))
                meet(sp, 3 * b + 3)
                sp.dma_start(wot[:, :, :], wo).then_inc(rows_in, 16)
                sp.dma_start(rows[:, 4], bo.partition_broadcast(P)).then_inc(rows_in, 16)
                for i, m in ((0, GA), (2, CB1), (3, SB)):
                    sp.dma_start(rows[:, i], modd[b, m * C:(m + 1) * C].partition_broadcast(P)).then_inc(rows_in, 16)
                with sp.Fori(0, NCH) as j:
                    ci = NCH * b + j
                    wait_apart(sp, y_ps, TPC * ci)
                    wait_apart(sp, x1_ready, ci)
                    for g in range(NG):
                        sp.dma_start(otc[:, g], otd[b, g, :, bass.ds(j * CH, CH)]).then_inc(c_in, 16)
                    sp.dma_start(xc[:, :, :], x[b, j].rearrange("(t p) c -> p t c", p=P)).then_inc(c_in, 16)
                    wait_apart(sp, x1_ready, ci + 1)
                    sp.dma_start(out[bass.ds(ci * CH, CH), :].rearrange("(t p) c -> p t c", p=P), x1[:, :, :]).then_inc(c_out, 16)
                    wait_apart(sp, h2_ready, ci + 1)
                    sp.dma_start(table[bass.ds(ci * CH, CH), 0:C].rearrange("(t p) c -> p t c", p=P), h2[:, :, :]).then_inc(c_out, 16)
                    wait_apart(sp, n_sb, ci + 1)
                    sp.dma_start(table[bass.ds(ci * CH, CH), C:ROW].rearrange("(t p) c -> p t c", p=P), gN[:, :, :]).then_inc(g_out, 16)
                wait_apart(sp, c_out, 128 * (b + 1))
                wait_apart(sp, g_out, 64 * (b + 1))
            meet(sp, 3 * NB + 1)
            wait_apart(sp, slots_sb, 1)
            for i in range(2):
                sp.dma_start(idxd[i].rearrange("(g p b) -> p g b", g=6, p=P), sidx[:, i]).then_inc(slots_out, 16)
            wait_apart(sp, slots_out, 32)

            def fetch(ee, u, first=False):
                if not first:
                    wait_apart(sp, scat, 64 * ee - 32 + 32 * u)
                    wait_apart(sp, d_ps, 4 * ee - 2 + 2 * u)
                for i in range(2):
                    sp.dma_start(it[:, u, i, :],
                                 idxd[i, bass.ds(ee * 512 + u * 256, CAP)].rearrange("(f p) -> p f", p=HALF),
                                 allow_slow_non_contiguous=True).then_inc(it_in[u], 16)
                sp.dma_start(Wg[:, u], wgu[2 * ee + u]).then_inc(we_in[u], 16)
                sp.dma_start(Wd[:, u], wdn[2 * ee + u]).then_inc(we_in[u], 16)

            fetch(0, 0, first=True)
            fetch(0, 1, first=True)
            with sp.Fori(1, NEW // 2) as ee:
                fetch(ee, 0)
                fetch(ee, 1)

        @block.gpsimd
        def _(pool):
            nc.gpsimd.memset(zrow[:, :], 0.0).then_inc(zero_ready, 1)
            nc.gpsimd.memset(tot[:, :], 0.0)
            nc.gpsimd.memset(Racc[:, :, :], 0.0)
            with pool.Fori(0, NB) as b:
                meet(pool, 3 * b + 1)
                with pool.Fori(0, NCH) as j:
                    wait_apart(pool, var_ready, NCH * b + j + 1)
                    nc.gpsimd.tensor_tensor(rsA[:, :], rsA[:, :], K[:, K_MH:K_MH + TPC], ALU.pow).then_inc(rs_done, 1)
                meet(pool, 3 * b + 2)
                nc.gpsimd.memset(QK[3 * HD:3 * HD + 1, :, 1, :].bitcast(F32), 1.0).then_inc(ones_set, 1)
                wait_apart(pool, ones_set, 3 * b + 1)
                nc.gpsimd.memset(part[:, :, :], -3e38).then_inc(ones_set, 1)
                nc.gpsimd.memset(V[:, :, :, HD:2 * HD], 1.0).then_inc(ones_set, 1)
                with pool.Fori(0, NG) as g:
                    gi = 4 * b + g
                    for j in range(NCH):
                        ck = NCH * gi + j
                        cols = slice(j * CH, (j + 1) * CH)
                        if j == 0:
                            pool.wait_ge(w_in, ONE + 32 * (b + 1) + 48 * (gi + 1))
                        pool.wait_ge(q_raw, ONE + 2 * ck + 2)
                        pool.wait_ge(q_lo, ONE + ck)
                        nc.gpsimd.tensor_tensor(t1[:, :, :], qraw[:, :, :], cs[:, 0:1, cols].broadcast_to([P, 2, CH]), ALU.mult).then_inc(rope_mul, 1)
                        pool.wait_ge(q_shuf, ONE + ck + 1)
                        nc.gpsimd.tensor_tensor(qs[:, :, :], qs[:, :, :], cs[:, 1:2, cols].broadcast_to([P, 2, CH]), ALU.mult).then_inc(rope_mul, 1)
                    wait_apart(pool, o_rec, NCH * GH * (gi + 1))
                    pool.wait_ge(den_inv, ONE + gi + 1)
                    nc.gpsimd.tensor_tensor(ot[:, :], ot[:, :], den[:, :], ALU.mult).then_inc(ot_ready, 1)
                meet(pool, 3 * b + 3)
                pool.wait_ge(rows_in, ONE + 80 * (b + 1))
                nc.gpsimd.tensor_tensor(rows[:, 1], rows[:, 0], rows[:, 4], ALU.mult).then_inc(gabo, 1)
                wait_apart(pool, gabo, b + 1)
                with pool.Fori(0, NCH) as j:
                    ci = NCH * b + j
                    pool.wait_ge(c_in, ONE + 80 * (ci + 1))
                    nc.gpsimd.tensor_tensor(xc[:, :, :], xc[:, :, :], rows[:, 1:2].broadcast_to([P, TPC, C]), ALU.add).then_inc(xg_ready, 1)
                    wait_apart(pool, varC_ready, ci + 1)
                    nc.gpsimd.tensor_tensor(rsC[:, :], rsC[:, :], K[:, K_MH:K_MH + TPC], ALU.pow).then_inc(rsC_done, 1)
            meet(pool, 3 * NB + 1)

            def gather(ee, u, first=False):
                wait_apart(pool, it_in[u], 32 * (ee + 1))
                if not first:
                    wait_apart(pool, z_ready, 4 * ee - 2 + 2 * u)
                for f in range(2):
                    pool.indirect_dma_start(X[:, u, f, :], None, table[:, :],
                                            bass.IndirectOffsetOnAxis(ap=it[:, u, 0, f:f + 1], axis=0)).then_inc(xg_in[u], 16)
                    pool.indirect_dma_start(GBr[:, u, f, :], None, gbd[:, :],
                                            bass.IndirectOffsetOnAxis(ap=it[:, u, 1, f:f + 1], axis=0)).then_inc(xg_in[u], 16)

            def scatter(ee, u, first=False):
                for f in range(2):
                    wait_apart(pool, z_ready, 4 * ee + 2 * u + f + 1)
                    if not (first and f == 0):
                        wait_apart(pool, scat, 64 * ee + 32 * u + 16 * f)
                    pool.indirect_dma_start(out[:, :], bass.IndirectOffsetOnAxis(ap=it[:, u, 0, f:f + 1], axis=0),
                                            z[:, u, f, :], None, compute_op=ALU.add).then_inc(scat, 16)

            gather(0, 0, first=True)
            gather(0, 1, first=True)
            scatter(0, 0, first=True)
            gather(1, 0)
            scatter(0, 1)
            with pool.Fori(1, NEW // 2 - 1) as ee:
                gather(ee, 1)
                scatter(ee, 0)
                gather(ee + 1, 0)
                scatter(ee, 1)
            gather(NEW // 2 - 1, 1)
            scatter(NEW // 2 - 1, 0)
            scatter(NEW // 2 - 1, 1)
            pool.wait_ge(scat, 32 * NEW)

        @block.scalar
        def _(act):
            act.wait_ge(consts_in, ONE + 96)
            nc.scalar.activation(ce[:, :, :], csT[:, :, :], ACT.Exp, scale=-1.0).then_inc(silu_e, 1)
            with act.Fori(0, NB) as b:
                meet(act, 3 * b + 1)
                with act.Fori(0, NCH) as j:
                    ci = NCH * b + j
                    act.wait_ge(hT_ps, ONE + ci + 1)
                    for ct in range(KT):
                        nc.scalar.activation(hT[:, ct, bass.ds(j * CH, CH)], PS[:, ct], ACT.Identity,
                                             bias=modc[:, b, ct:ct + 1], scale=modc[:, b, KT + ct:KT + ct + 1]).then_inc(hT_sb, 1)
                meet(act, 3 * b + 2)
                with act.Fori(0, NG) as g:
                    gi = 4 * b + g
                    act.wait_ge(w_in, ONE + 32 * (b + 1) + 48 * (gi + 1))
                    act.wait_ge(pv_done, ONE + NS2 * gi)
                    for j in range(NCH):
                        ck = NCH * gi + j
                        for i in range(2):
                            act.wait_ge(qk_ps, ONE + 2 * ck + i + 1)
                            act.wait_ge(rope_add, ONE + ck)
                            nc.scalar.activation(qraw[:, i], S2[j % 2][:, i], ACT.Identity, bias=bqg[:, i:i + 1]).then_inc(q_raw, 1)
                        act.wait_ge(rope_add, ONE + ck + 1)
                        if j >= 2:
                            act.wait_ge(qk_in[j % 2], ONE + 384 * gi + 192)
                        else:
                            act.wait_ge(qk_in[j % 2], ONE + 384 * gi)
                        nc.scalar.activation(st[:, j % 2, 0::2], t1[:, :, :], ACT.Copy).then_inc(q_hi, 1)
                    act.wait_ge(q_lo, ONE + NCH * (gi + 1))
                    for h in range(GH):
                        for u, (j, kb, q0, diag) in enumerate(UNITS):
                            n = NU * h + u
                            act.wait_ge(s2_ready, ONE + NS2 * gi + n + 1)
                            if n >= 4:
                                act.wait_ge(pv_done, ONE + NS2 * gi + n - 3)
                            nc.scalar.activation(Pr[:, n % 4, :, q0:CH], S2[n % 2][:, :, q0:CH], ACT.Exp, scale=SCALE).then_inc(exp_done, 1)
                meet(act, 3 * b + 3)
                with act.Fori(0, NCH) as j:
                    ci = NCH * b + j
                    for t in range(TPC):
                        act.wait_ge(t_ps, ONE + TPC * ci + t + 1)
                        nc.scalar.activation(h2T[:, :, t * P:(t + 1) * P], PS[:, 2].rearrange("p (c q) -> p c q", c=KT), ACT.Copy).then_inc(t_sb, 1)
                    act.wait_ge(key_ready, ONE + ci + 1)
                    nc.scalar.activation(ex[:, :, :], key[:, :, :], ACT.Exp).then_inc(ex_ready, 1)
                    act.wait_ge(gt_ps, ONE + 2 * ci + 1)
                    nc.scalar.activation(gT[:, :, :], PS[:, 2].rearrange("p (c q) -> p c q", c=TPC), ACT.Copy).then_inc(gt_sb, 1)
                    act.wait_ge(gt_ps, ONE + 2 * ci + 2)
                    nc.scalar.activation(mTb[:, :, :], PS[:, 2].rearrange("p (c q) -> p c q", c=TPC), ACT.Copy).then_inc(gt_sb, 1)
            meet(act, 3 * NB + 1)

            def xt_copy(n):
                for i in range(2):
                    act.wait_ge(xt_ps, ONE + 2 * n + i + 1)
                    act.wait_ge(gu_ps, ONE + 2 * n)
                    nc.scalar.activation(XT[:, i], PS[:, i, 0:2 * CAP].rearrange("p (k s) -> p k s", k=2), ACT.Copy).then_inc(xt_sb, 1)

            def exp_gate(e):
                act.wait_ge(gu_ps, ONE + 2 * e + 1)
                act.wait_ge(h_ready, ONE + e)
                nc.scalar.activation(e1[:, :, :], PS[0:HALF, 2, 0:2 * CAP].rearrange("p (k s) -> p k s", k=2), ACT.Exp, scale=-1.0).then_inc(e_ready, 1)

            xt_copy(0)
            with act.Fori(0, NEW - 1) as e:
                exp_gate(e)
                xt_copy(e + 1)
            exp_gate(NEW - 1)

        @block.tensor
        def _(pe):
            mm = nc.tensor.matmul
            pe.wait_ge(cs_ready, ONE + 1)
            for m in range(6):
                for k in range(KT):
                    last = mm(PS[0:NB, m], csT[:, k, :], wm[:, k, m * C:(m + 1) * C], start=k == 0, stop=k == KT - 1)
                last.then_inc(mod_ps, 1)
            pe.wait_ge(mod_done, ONE + 1)
            for i in range(2 * KT):
                m, ct = (SA, i) if i < KT else (CA1, i - KT)
                last = nc.tensor.transpose(PS[:, 6, i * NB:(i + 1) * NB], mods[:, m * C + ct * P:m * C + (ct + 1) * P], K[0:NB, K_ID:K_ID + NB])
            last.then_inc(modT_ps, 1)

            order = schedule()
            with pe.Fori(0, NB) as b:
                meet(pe, 3 * b + 1)
                with pe.Fori(0, NCH) as j:
                    ci = NCH * b + j
                    pe.wait_ge(hT_sb, ONE + KT * ci)
                    for t in range(TPC):
                        pe.wait_ge(xhat_ready, ONE + TPC * ci + t + 1)
                        for ct in range(KT):
                            last = nc.tensor.transpose(PS[:, ct, t * P:(t + 1) * P], xhat[:, t, ct * P:(ct + 1) * P], ident)
                    last.then_inc(hT_ps, 1)
                meet(pe, 3 * b + 2)
                wait_apart(pe, ones_set, 3 * (b + 1))
                with pe.Fori(0, NG) as g:
                    gi = 4 * b + g
                    pe.wait_ge(w_in, ONE + 32 * (b + 1) + 48 * (gi + 1))
                    for j in range(NCH):
                        cols = slice(j * CH, (j + 1) * CH)
                        pe.wait_ge(q_raw, ONE + 2 * (NCH * gi + max(j - 1, 0)))
                        for i in range(2):
                            for k in range(KT):
                                last = mm(S2[j % 2][:, i], W[:, k, i * P:(i + 1) * P], hT[:, k, cols], start=k == 0, stop=k == KT - 1)
                            last.then_inc(qk_ps, 1)
                        pe.wait_ge(v_sb, ONE + NCH * gi + max(j - 1, 0))
                        for t in range(TPC):
                            for k in range(KT):
                                last = mm(S1[j % 2][:, t * P:(t + 1) * P], hT[:, k, j * CH + t * P:j * CH + (t + 1) * P],
                                          W[:, k, 2 * P:3 * P], start=k == 0, stop=k == KT - 1)
                        last.then_inc(v_ps, 1)
                    pe.wait_ge(v_sb, ONE + NCH * (gi + 1))
                    for i in range(2):
                        pe.wait_ge(qk_in[i], ONE + 384 * (gi + 1))
                    n1 = 0
                    for step in order:
                        kind, h = step[:2]
                        if kind == "max":
                            qb, c, w = TILES[step[2]]
                            pe.wait_ge(s1_free, ONE + NS1 * gi + max(n1 - 1, 0))
                            mm(S1[n1 % 2][:, 0:w], QK[0:3 * HD, h, 0, qb * P:(qb + 1) * P], QK[0:3 * HD, h, 1, c * CH:c * CH + w],
                               start=True, stop=True).then_inc(s1_ready, 1)
                            n1 += 1
                        elif kind == "row":
                            pe.wait_ge(max_all, ONE + GH * gi + h + 1)
                            pe.wait_ge(s1_free, ONE + NS1 * gi + max(n1 - 1, 0))
                            nc.tensor.transpose(S1[n1 % 2][0:NT, 0:P], mx[:, :], ident).then_inc(s1_ready, 1)
                            n1 += 1
                        elif kind == "score":
                            u = step[2]
                            j, kb, q0, diag = UNITS[u]
                            n = NU * h + u
                            if u == 0:
                                pe.wait_ge(mrow_in, ONE + 16 * (GH * gi + h + 1))
                            pe.wait_ge(exp_done, ONE + NS2 * gi + max(n - 1, 0))
                            for i in range(2):
                                last = mm(S2[n % 2][:, i, q0:CH], QK[0:3 * HD + 1, h, 1, (kb + i) * P:(kb + i + 1) * P],
                                          QK[0:3 * HD + 1, h, 0, j * CH + q0:(j + 1) * CH], start=True, stop=not diag)
                                if diag:
                                    last = mm(S2[n % 2][:, i, q0:q0 + (i + 1) * P], idbf[:, :], mtbf[:, (1 - i) * P:2 * P], start=False, stop=True)
                            last.then_inc(s2_ready, 1)
                        elif kind == "value":
                            u = step[2]
                            j, kb, q0, diag = UNITS[u]
                            n = NU * h + u
                            pe.wait_ge(exp_done, ONE + NS2 * gi + n + 1)
                            if kb == 0:
                                pe.wait_ge(o_norm, ONE + NCH * GH * gi + max(NCH * h + j - 1, 0))
                            for i in range(2):
                                r = max(kb + i - TPC * j, 0)
                                last = mm(O[j % 2][0:2 * HD, r * P:CH], V[:, kb + i, h, :], Pr[:, n % 4, i, r * P:CH],
                                          start=kb + i == 0, stop=kb + i == TPC * (j + 1) - 1)
                            last.then_inc(pv_done, 1)
                meet(pe, 3 * b + 3)
                wait_apart(pe, rows_in, 80 * (b + 1))
                with pe.Fori(0, NCH) as j:
                    ci = NCH * b + j
                    pe.wait_ge(c_in, ONE + 80 * (ci + 1))
                    for t in range(TPC):
                        pe.wait_ge(y_used, ONE + TPC * ci + max(t - 1, 0))
                        for k in range(KT):
                            last = mm(PS[:, t % 2], otc[:, k, t * P:(t + 1) * P], wot[:, k, :], start=k == 0, stop=k == KT - 1)
                        last.then_inc(y_ps, 1)
                    pe.wait_ge(h2_ready, ONE + ci + 1)
                    for t in range(TPC):
                        if t == 0:
                            pe.wait_ge(gt_sb, ONE + 2 * ci)
                        pe.wait_ge(t_sb, ONE + TPC * ci + t)
                        for ct in range(KT):
                            last = nc.tensor.transpose(PS[:, 2, ct * P:(ct + 1) * P], h2[:, t, ct * P:(ct + 1) * P], ident)
                        last.then_inc(t_ps, 1)
                    pe.wait_ge(t_sb, ONE + TPC * (ci + 1))
                    pe.wait_ge(pos_ready, ONE + ci)
                    for t in range(TPC):
                        for ct in range(KT):
                            last = mm(PS[:, 3, t * NOLD:(t + 1) * NOLD], h2T[:, ct, t * P:(t + 1) * P], gwt[:, ct, :], start=ct == 0, stop=ct == KT - 1)
                    last.then_inc(l_ps, 1)
                    pe.wait_ge(g_ready, ONE + ci + 1)
                    for i, src in enumerate((ex, msk)):
                        pe.wait_ge(gt_sb, ONE + 2 * ci + i)
                        for t in range(TPC):
                            last = nc.tensor.transpose(PS[:, 2, t * P:(t + 1) * P], src[:, t, :], ident)
                        last.then_inc(gt_ps, 1)
                    pe.wait_ge(gt_sb, ONE + 2 * ci + 2)
                    pe.wait_ge(n_sb, ONE + ci)
                    for t in range(TPC):
                        mm(PS[:, 4, t * 96:t * 96 + NEW], gT[:, t, :], Mold[:, :], start=True, stop=True)
                        last = mm(PS[:, 4, t * 96 + NEW:t * 96 + 96], mTb[:, t, :], Mbf[:, :], start=True, stop=True)
                    last.then_inc(n_ps, 1)
                    pe.wait_ge(n_sb, ONE + ci + 1)
                    for t in range(TPC + 1):
                        o = PS[:, 3, t * NEW:(t + 1) * NEW]
                        for s in range(t):
                            last = mm(o, onesbf[:, :], mN[:, s, :], start=s == 0, stop=t == TPC and s == t - 1)
                        if t < TPC:
                            last = mm(o, Ubf[:, :], mN[:, t, :], start=t == 0, stop=True)
                    last.then_inc(p_ps, 1)
                    pe.wait_ge(ab_ready, ONE + ci + 1)
                    pe.wait_ge(r_sb, ONE + ci)
                    for g in range(6):
                        for t in range(TPC):
                            last = mm(PS[:, 5 + g // 2, (g % 2) * 256:(g % 2 + 1) * 256],
                                      Aoh[:, t, 8 * g:8 * g + 8, :].rearrange("p e a -> p (e a)"),
                                      B2[:, t, g].rearrange("p v c -> p (v c)"), start=t == 0, stop=t == TPC - 1)
                    last.then_inc(r_ps, 1)
            meet(pe, 3 * NB + 1)

            def turn(n, u, ee):
                pe.wait_ge(xg_in[u], 64 * (ee + 1))
                pe.wait_ge(xt_sb, ONE + 2 * n)
                for i in range(2):
                    for kk in range(2):
                        for f in range(2):
                            ct = 2 * i + kk
                            last = nc.tensor.transpose(PS[:, i, kk * CAP + f * HALF:kk * CAP + (f + 1) * HALF],
                                                       X[:, u, f, ct * P:(ct + 1) * P], K[0:HALF, K_ID:K_ID + HALF])
                    last.then_inc(xt_ps, 1)

            def gate_up(n, u, ee):
                pe.wait_ge(xt_sb, ONE + 2 * n + 2)
                pe.wait_ge(we_in[u], ONE + 32 * (ee + 1))
                pe.wait_ge(h_ready, ONE + n)
                for i in range(2):
                    for q in range(2):
                        for k in range(KT):
                            o = (2 * i + q) * HALF
                            last = mm(PS[0:HALF, 2 + i, q * CAP:(q + 1) * CAP], Wg[:, u, k, o:o + HALF], XT[:, k // 2, k % 2, :],
                                      start=k == 0, stop=k == KT - 1)
                    last.then_inc(gu_ps, 1)

            def down(n, u, ee):
                pe.wait_ge(h_ready, ONE + n + 1)
                for f in range(2):
                    pe.wait_ge(z_ready, ONE + 2 * n)
                    for q in range(2):
                        last = mm(PS[0:HALF, 4 + f, :], hb[:, q, f * HALF:(f + 1) * HALF], Wd[:, u, q, :], start=q == 0, stop=q == 1)
                    last.then_inc(d_ps, 1)

            turn(0, 0, 0)
            with pe.Fori(0, NEW // 2 - 1) as ee:
                gate_up(2 * ee, 0, ee)
                turn(2 * ee + 1, 1, ee)
                down(2 * ee, 0, ee)
                gate_up(2 * ee + 1, 1, ee)
                turn(2 * ee + 2, 0, ee + 1)
                down(2 * ee + 1, 1, ee)
            ee = NEW // 2 - 1
            gate_up(2 * ee, 0, ee)
            turn(2 * ee + 1, 1, ee)
            down(2 * ee, 0, ee)
            gate_up(2 * ee + 1, 1, ee)
            down(2 * ee + 1, 1, ee)

        @block.vector
        def _(dve):
            v = nc.vector
            pre = Chain(dve, prep, 20)
            pre.begin(0)
            dve.wait_ge(consts_in, ONE + 96)
            dve.wait_ge(silu_e, ONE + 1)
            pre.link(v.tensor_scalar(ce[:, :, :], ce[:, :, :], 1.0, None, ALU.add))
            pre.link(v.reciprocal(ce[:, :, :], ce[:, :, :]))
            v.tensor_tensor(csT[:, :, :], csT[:, :, :], ce[:, :, :], ALU.mult).then_inc(cs_ready, 1)
            v.tensor_copy(Ubf[:, :], K[:, K_U:K_U + P])
            v.tensor_copy(onesbf[:, :], K[:, K_ONE:K_ONE + P])
            v.tensor_copy(idbf[:, :], K[:, K_ID:K_ID + P])
            v.tensor_copy(mtbf[:, :], K[:, K_MT:K_MT + 2 * P])
            v.tensor_copy(tcol[:, :], K[:, K_T4:K_T4 + TPC])
            pre.link(v.tensor_copy(ocf[:, :], oc[:, :]))
            pre.link(v.tensor_scalar(Mold[:, :], K[:, K_I48:K_I48 + NEW], ocf[:, :], None, ALU.is_equal))
            v.tensor_copy(Mbf[:, :], Mold[:, :])
            pre.link(v.tensor_copy(negb[:, :], orow[:, :]))
            pre.link(v.tensor_scalar(negb[:, :], negb[:, :], -1.0, NEG, ALU.is_equal, ALU.mult))
            for m in range(6):
                dve.wait_ge(mod_ps, ONE + m + 1)
                dst = mods[:, m * C:(m + 1) * C]
                if m in (CA1, CB1):
                    pre.link(v.tensor_scalar(dst, PS[0:NB, m], 1.0, None, ALU.add))
                elif m in (GA, GB):
                    pre.link(v.tensor_scalar(sgn[:, :], PS[0:NB, m], 0.0, 2.0, ALU.is_ge, ALU.mult))
                    pre.link(v.tensor_scalar(sgn[:, :], sgn[:, :], 1.0, None, ALU.subtract))
                    pre.link(v.tensor_tensor(dst, PS[0:NB, m], sgn[:, :], ALU.mult))
                    pre.link(v.tensor_scalar(dst, dst, 0.25, None, ALU.max))
                    if m == GB:
                        v.tensor_tensor(dst, dst, sgn[:, :], ALU.mult).then_inc(mod_done, 1)
                    else:
                        pre.link(v.tensor_tensor(dst, dst, sgn[:, :], ALU.mult))
                else:
                    pre.link(v.tensor_copy(dst, PS[0:NB, m]))
            dve.wait_ge(modT_ps, ONE + 1)
            pre.link(v.tensor_copy(modc[:, :, :].rearrange("p b k -> p k b"), PS[:, 6, 0:2 * KT * NB].rearrange("p (k b) -> p k b", b=NB)))
            pre.end()

            a = Chain(dve, chA, 2)
            c = Chain(dve, chC, 19)
            order = schedule()
            with dve.Fori(0, NB) as b:
                meet(dve, 3 * b + 1)
                with dve.Fori(0, NCH // 2) as jj:
                    for u in range(2):
                        ci = NCH * b + 2 * jj + u
                        a.begin(ci)
                        dve.wait_ge(x_in[u], ONE + 32 * b + 16 * jj + 16)
                        for t in range(TPC):
                            last = v.bn_stats(stA[:, t, :], xin[:, u, t, :])
                        a.link(last, passed)
                        for t in range(TPC):
                            last = v.bn_aggr(mvA[:, t, :], stA[:, t, :])
                        a.link(last)
                        v.tensor_scalar(rsA[:, :], mvA[:, :, 1], EPS, None, ALU.add).then_inc(var_ready, 1)
                        dve.wait_ge(rs_done, ONE + ci + 1)
                        dve.wait_ge(hT_ps, ONE + ci)
                        for t in range(TPC):
                            last = v.tensor_scalar(xhat[:, t, :], xin[:, u, t, :], mvA[:, t, 0:1], rsA[:, t:t + 1], ALU.subtract, ALU.mult)
                            last.then_inc(xhat_ready, 1)
                        a.end()
                meet(dve, 3 * b + 2)
                wait_apart(dve, ones_set, 3 * (b + 1))
                with dve.Fori(0, NG) as g:
                    gi = 4 * b + g
                    dve.wait_ge(w_in, ONE + 32 * (b + 1) + 48 * (gi + 1))
                    for j in range(NCH):
                        ck = NCH * gi + j
                        swap = list(range(HD // 2, HD)) + list(range(HD // 2))
                        wait_apart(dve, q_raw, 2 * ck + 2)
                        v.stream_shuffle(qs[:, :, :], qraw[:, :, :], swap).then_inc(q_shuf, 1)
                        dve.wait_ge(v_ps, ONE + ck + 1)
                        v.tensor_tensor(V[:, TPC * j:TPC * (j + 1), :, 0:HD],
                                        S1[j % 2].rearrange("p (t h d) -> p t h d", t=TPC, h=GH),
                                        bvg[:, :].rearrange("p (h d) -> p h d", h=GH).unsqueeze(1).broadcast_to([P, TPC, GH, HD]),
                                        ALU.add).then_inc(v_sb, 1)
                        dve.wait_ge(rope_mul, ONE + 2 * ck + 2)
                        v.tensor_tensor(t1[:, :, :], t1[:, :, :], qs[:, :, :], ALU.add).then_inc(rope_add, 1)
                        dve.wait_ge(q_hi, ONE + ck + 1)
                        dve.wait_ge(rope_add, ONE + ck + 1)
                        v.tensor_tensor(st[:, j % 2, 1::2], t1[:, :, :], st[:, j % 2, 0::2], ALU.subtract).then_inc(q_lo, 1)
                    n1 = 0
                    for step in order:
                        kind, h = step[:2]
                        if kind == "max":
                            qb, cc, w = TILES[step[2]]
                            wait_apart(dve, s1_ready, NS1 * gi + n1 + 1)
                            if cc == qb // TPC:
                                v.tensor_tensor_reduce(out=S1[n1 % 2][:, 0:w], in0=S1[n1 % 2][:, 0:w], in1=K[:, K_NEG + CH - w:K_NEG + CH],
                                                       scale=1.0, scalar=-3e38, op0=ALU.add, op1=ALU.max,
                                                       accum_out=part[:, qb, cc:cc + 1]).then_inc(s1_free, 1)
                            else:
                                v.reduce_max(part[:, qb, cc:cc + 1], S1[n1 % 2][:, 0:w], AX.X).then_inc(s1_free, 1)
                            n1 += 1
                        elif kind == "row":
                            dve.wait_ge(s1_free, ONE + NS1 * gi + n1)
                            v.reduce_max(mx[:, :], part[:, :, :], AX.X).then_inc(max_all, 1)
                            dve.wait_ge(mrow_in, ONE + 16 * (GH * gi + h))
                            dve.wait_ge(s1_ready, ONE + NS1 * gi + n1 + 1)
                            v.tensor_scalar(mT[:, :], S1[n1 % 2][0:NT, 0:P], -1.0, None, ALU.mult).then_inc(s1_free, 1)
                            n1 += 1
                        elif kind == "norm":
                            j = step[2]
                            nn = NCH * h + j
                            last_u = max(u for u in range(NU) if UNITS[u][0] == j)
                            dve.wait_ge(pv_done, ONE + NS2 * gi + NU * h + last_u + 1)
                            if nn == 0:
                                dve.wait_ge(ot_out, ONE + 16 * gi)
                            own, cols = slice(h * HD, (h + 1) * HD), slice(j * CH, (j + 1) * CH)
                            v.tensor_copy(ot[own, cols], O[j % 2][0:HD, :]).then_inc(o_rec, 1)
                            v.tensor_copy(den[own, cols], O[j % 2][HD:2 * HD, :]).then_inc(o_norm, 1)
                    dve.wait_ge(o_norm, ONE + NCH * GH * (gi + 1))
                    v.reciprocal(den[:, :], den[:, :]).then_inc(den_inv, 1)
                meet(dve, 3 * b + 3)
                wait_apart(dve, rows_in, 80 * (b + 1))
                with dve.Fori(0, NCH) as j:
                    ci = NCH * b + j
                    c.begin(ci)
                    dve.wait_ge(c_out, ONE + 32 * ci)
                    for t in range(TPC):
                        dve.wait_ge(y_ps, ONE + TPC * ci + t + 1)
                        v.tensor_tensor(x1[:, t, :], PS[:, t % 2], rows[:, 0], ALU.mult).then_inc(y_used, 1)
                    dve.wait_ge(y_used, ONE + TPC * (ci + 1))
                    dve.wait_ge(xg_ready, ONE + ci + 1)
                    v.tensor_tensor(x1[:, :, :], x1[:, :, :], xc[:, :, :], ALU.add).then_inc(x1_ready, 1)
                    dve.wait_ge(x1_ready, ONE + ci + 1)
                    for t in range(TPC):
                        last = v.bn_stats(stC[:, t, :], x1[:, t, :])
                    c.link(last, passed)
                    for t in range(TPC):
                        last = v.bn_aggr(mvC[:, t, :], stC[:, t, :])
                    c.link(last)
                    v.tensor_scalar(rsC[:, :], mvC[:, :, 1], EPS, None, ALU.add).then_inc(varC_ready, 1)
                    
                    for t in range(TPC):
                        last = v.scalar_tensor_tensor(h2[:, t, :], x1[:, t, :], mvC[:, t, 0:1], rows[:, 2], ALU.subtract, ALU.mult)
                    c.link(last)
                    dve.wait_ge(rsC_done, ONE + ci + 1)
                    for t in range(TPC):
                        last = v.scalar_tensor_tensor(h2[:, t, :], h2[:, t, :], rsC[:, t:t + 1], rows[:, 3], ALU.mult, ALU.add)
                    last.then_inc(h2_ready, 1)
                    dve.wait_ge(l_ps, ONE + ci + 1)
                    c.link(v.tensor_tensor(key[:, :, :], PS[:, 3].rearrange("p (t e) -> p t e", t=TPC),
                                           negb[:, :].unsqueeze(1).broadcast_to([P, TPC, NOLD]), ALU.add))
                    c.link(v.reduce_max(lmx[:, :], key[:, :, :], AX.X))
                    v.tensor_tensor(key[:, :, :], key[:, :, :], lmx[:, :].unsqueeze(2).broadcast_to([P, TPC, NOLD]), ALU.subtract).then_inc(key_ready, 1)
                    dve.wait_ge(key_ready, ONE + ci + 1)
                    c.link(v.tensor_scalar(rep[:, :, :], key[:, :, :], FLOOR, None, ALU.max), passed)
                    for t in range(TPC):
                        last = v.max(top[:, t, :], rep[:, t, :])
                    c.link(last, passed)
                    for t in range(TPC):
                        last = v.match_replace(msk[:, t, :], top[:, t, :], rep[:, t, :], -3e38)
                    c.link(last)
                    c.link(v.tensor_scalar(msk[:, :, :], msk[:, :, :], -1e38, None, ALU.is_lt))
                    dve.wait_ge(ex_ready, ONE + ci + 1)
                    c.link(v.tensor_tensor(ex[:, :, :], ex[:, :, :], msk[:, :, :], ALU.mult))
                    c.link(v.reduce_sum(gs[:, :], ex[:, :, :], AX.X))
                    c.link(v.reciprocal(gs[:, :], gs[:, :]))
                    v.tensor_tensor(ex[:, :, :], ex[:, :, :], gs[:, :].unsqueeze(2).broadcast_to([P, TPC, NOLD]), ALU.mult).then_inc(g_ready, 1)
                    dve.wait_ge(n_ps, ONE + ci + 1)
                    dve.wait_ge(g_out, ONE + 16 * ci)
                    pn = PS[:, 4, 0:TPC * 96].rearrange("p (t v e) -> p t v e", t=TPC, v=2)
                    v.tensor_copy(gN[:, :, :], pn[:, :, 0, :])
                    v.tensor_copy(mN[:, :, :], pn[:, :, 1, :]).then_inc(n_sb, 1)
                    dve.wait_ge(p_ps, ONE + ci + 1)
                    dve.wait_ge(n_sb, ONE + ci + 1)
                    c.link(v.tensor_tensor(pos[:, :, :], PS[:, 3, 0:TPC * NEW].rearrange("p (t e) -> p t e", t=TPC),
                                           tot[:, :].unsqueeze(1).broadcast_to([P, TPC, NEW]), ALU.add))
                    c.link(v.tensor_tensor(tot[:, :], tot[:, :], PS[:, 3, TPC * NEW:(TPC + 1) * NEW], ALU.add))
                    c.link(v.scalar_tensor_tensor(pos[:, :, :], mN[:, :, :], -BIG, pos[:, :, :], ALU.mult, ALU.add))
                    c.link(v.tensor_scalar(posi[:, :, :], pos[:, :, :], BIG, None, ALU.add))
                    v.tensor_scalar(lo[:, :, :], posi[:, :, :], 15, None, ALU.bitwise_and).then_inc(pos_ready, 1)
                    c.link(v.tensor_scalar(hi[:, :, :], posi[:, :, :], 0xFFFFF0, None, ALU.bitwise_and))
                    v.tensor_tensor(Aoh[:, :, :, :].rearrange("p t e a -> p (t e) a"),
                                    hi[:, :, :].rearrange("p t e -> p (t e)").unsqueeze(2).broadcast_to([P, TPC * NEW, 16]),
                                    K[:, K_A16:K_A16 + 16].unsqueeze(1).broadcast_to([P, TPC * NEW, 16]), ALU.is_equal)
                    dve.wait_ge(pos_ready, ONE + ci + 1)
                    c.link(v.tensor_tensor(B1[:, :, :, :].rearrange("p t g (e b) -> p (t g e) b", b=16),
                                           lo[:, :, :].rearrange("p t e -> p (t e)").unsqueeze(2).broadcast_to([P, TPC * NEW, 16]),
                                           K[:, K_B16:K_B16 + 16].unsqueeze(1).broadcast_to([P, TPC * NEW, 16]), ALU.is_equal))
                    v.tensor_scalar(B2[:, :, :, 0, :].rearrange("p t g c -> p (t g) c"), B1[:, :, :, :].rearrange("p t g c -> p (t g) c"), K[:, K_P1:K_P1 + 1], None, ALU.mult)
                    for t in range(TPC):
                        last = v.tensor_scalar(B2[:, t, :, 1, :], B1[:, t, :, :], tcol[:, t:t + 1], None, ALU.mult)
                    last.then_inc(ab_ready, 1)
                    dve.wait_ge(ab_ready, ONE + ci + 1)
                    c.link(v.tensor_scalar(tcol[:, :], tcol[:, :], float(TPC), None, ALU.add))
                    dve.wait_ge(r_ps, ONE + ci + 1)
                    v.tensor_tensor(Racc[:, :, :].rearrange("p (b g) c -> p b (g c)", g=2), Racc[:, :, :].rearrange("p (b g) c -> p b (g c)", g=2),
                                    PS[:, 5:8], ALU.add).then_inc(r_sb, 1)
                    dve.wait_ge(r_sb, ONE + ci + 1)
                    c.end()
            meet(dve, 3 * NB + 1)
            d = Chain(dve, chD, 8)
            d.begin(0)
            d.link(v.tensor_tensor(Rd[:, :, :, :, :].rearrange("p g v e b -> p (g v) e b"),
                                   Racc[:, :, :].rearrange("p g (v e b) -> p (g v) e b", v=2, e=8),
                                   K[:, K_BD:K_BD + 8].unsqueeze(1).unsqueeze(3).broadcast_to([P, 12, 8, 16]), ALU.mult))
            d.link(v.reduce_sum(slot[:, :, :, :].rearrange("p g v b -> p (g v) b"),
                                Rd[:, :, :, :, :].rearrange("p g v e b -> p (g v) b e"), AX.X))
            d.link(v.scalar_tensor_tensor(tok1[:, :, :], slot[:, :, 1, :], float(P), slot[:, :, 0, :], ALU.mult, ALU.add))
            d.link(v.tensor_scalar(emp[:, :, :], tok1[:, :, :], 0.0, None, ALU.is_equal))
            d.link(v.tensor_tensor(emp[:, :, :], emp[:, :, :], K[:, K_DUM:K_DUM + 16].unsqueeze(1).broadcast_to([P, 6, 16]), ALU.mult))
            d.link(v.tensor_tensor(tok1[:, :, :], tok1[:, :, :], emp[:, :, :], ALU.add))
            d.link(v.tensor_scalar(sidx[:, 0], tok1[:, :, :], 1.0, None, ALU.subtract))
            d.link(v.tensor_scalar(sidx[:, 1], sidx[:, 0], 11, None, ALU.logical_shift_right))
            dve.sem_inc(slots_sb, 1)
            d.end()

            ch = Chain(dve, chE, 3)

            def expert(ee, first=False):
                for u in range(2):
                    e = 2 * ee + u
                    ch.begin(e)
                    g2 = PS[0:HALF, 2, 0:2 * CAP].rearrange("p (k s) -> p k s", k=2)
                    u2 = PS[0:HALF, 3, 0:2 * CAP].rearrange("p (k s) -> p k s", k=2)
                    dve.wait_ge(e_ready, ONE + e + 1)
                    ch.link(v.tensor_scalar(e1[:, :, :], e1[:, :, :], 1.0, None, ALU.add))
                    ch.link(v.reciprocal(e1[:, :, :], e1[:, :, :]))
                    ch.link(v.tensor_tensor(e1[:, :, :], e1[:, :, :], g2, ALU.mult))
                    dve.wait_ge(gu_ps, ONE + 2 * e + 2)
                    dve.wait_ge(d_ps, ONE + 2 * e)
                    v.tensor_tensor(hb[:, :, :], e1[:, :, :], u2, ALU.mult).then_inc(h_ready, 1)
                    dve.wait_ge(xg_in[u], 64 * (ee + 1))
                    v.tensor_copy(wv[:, u, :], X[:, u, :, bass.ds(C + 2 * ee + u, 1)].rearrange("p f o -> p (f o)")).then_inc(wv_ready, 1)
                    dve.wait_ge(wv_ready, ONE + e + 1)
                    if not first:
                        dve.wait_ge(scat, 64 * ee - 32 + 32 * u)
                    for f in range(2):
                        dve.wait_ge(d_ps, ONE + 2 * e + f + 1)
                        v.scalar_tensor_tensor(z[:, u, f, :], PS[0:HALF, 4 + f, :], wv[:, u, f:f + 1], GBr[:, u, f, :], ALU.mult, ALU.mult).then_inc(z_ready, 1)
                    ch.end()

            expert(0, first=True)
            with dve.Fori(1, NEW // 2) as ee:
                expert(ee)


_INS = ("x", "wqkv", "bqk", "bv", "wo", "bo", "cT", "wmod", "gwT", "o2n_col", "o2n_row", "wgu", "wdn", "cos", "sin", "kst")


def laid_out(L0_attn_x, L0_attn_Wqkv, L0_attn_bqkv, L0_attn_Wo, L0_attn_bo, L0_ffn_gate_weight, L0_ffn_gate_up_proj,
             L0_ffn_down_proj, L0_ffn_old_to_new, L0_c, L0_wmod):
    def rows_first(w, n):
        return w.reshape(-1, P, n).transpose(1, 0, 2)

    w3 = np.asarray(L0_attn_Wqkv).reshape(3, NG, P, KT, P)
    b3 = np.asarray(L0_attn_bqkv).reshape(3, NG, P)
    cos, sin = rope_tables()
    gu = np.asarray(L0_ffn_gate_up_proj).transpose(0, 2, 1).reshape(NEW, KT, P, 2 * INTER)
    dn = np.asarray(L0_ffn_down_proj).transpose(0, 2, 1).reshape(NEW, 2, HALF, C)
    a = {
        "x": np.asarray(L0_attn_x).reshape(NB, NCH, CH, C),
        "wqkv": w3.transpose(1, 4, 3, 0, 2).reshape(NG, P, KT, 3 * P),
        "bqk": b3[:2].transpose(1, 2, 0),
        "bv": b3[2],
        "wo": rows_first(np.asarray(L0_attn_Wo).T, C),
        "bo": np.asarray(L0_attn_bo),
        "cT": rows_first(np.asarray(L0_c).T, NB),
        "wmod": rows_first(np.asarray(L0_wmod), 6 * C),
        "gwT": rows_first(np.asarray(L0_ffn_gate_weight).T, NOLD),
        "o2n_col": np.asarray(L0_ffn_old_to_new).reshape(NOLD, 1),
        "o2n_row": np.asarray(L0_ffn_old_to_new),
        "wgu": gu.transpose(0, 2, 1, 3),
        "wdn": dn.transpose(0, 2, 1, 3),
        "cos": cos, "sin": sin, "kst": constants(),
    }
    return {k: np.ascontiguousarray(v) for k, v in a.items()}


def kernel(**inputs):
    from concourse import bacc
    from concourse.bass_utils import run_bass_kernel_spmd

    nc = bacc.Bacc("TRN2", target_bir_lowering=False, num_devices=1)
    arrays = laid_out(**inputs)
    args = [nc.dram_tensor(n, arrays[n].shape, mybir.dt.from_np(arrays[n].dtype), kind="ExternalInput").ap() for n in _INS]
    out = nc.dram_tensor("out", (NROW, C), F32, kind="ExternalOutput").ap()
    adaln_block(nc, *args, out)
    r = run_bass_kernel_spmd(nc, [arrays], core_ids=[0])
    return r.results[0]["out"][:NTOK].reshape(NB, T, C)
```

```python
from contextlib import ExitStack

import numpy as np

import concourse.bass as bass
from concourse import mybir

F32 = mybir.dt.float32
F32R = mybir.dt.float32r
BF16 = mybir.dt.bfloat16
I32 = mybir.dt.int32
ALU = mybir.AluOpType
ACT = mybir.ActivationFunctionType
AX = mybir.AxisListType

P = 128
NB, T, C, H, HD = 4, 2048, 512, 16, 32
KT = C // P
CH = 512
NCH = T // CH
TPC = CH // P
NT = T // P
GH = P // HD
NG = H // GH
NTOK = NB * T
NOLD, NEW, TOPK = 128, 48, 8
CAP, INTER = 192, 192
HALF = CAP // 2
ROW = C + NEW
NROW = NTOK + HALF
EPS = 1e-5
SCALE = float(HD) ** -0.5
NEG = -1e30
FLOOR = -104.0
TURN, HELD = 8, 4
BIG = 16384.0
SA, CA1, GA, SB, CB1, GB = range(6)

K_ID, K_NEG, K_U, K_ONE = 0, 128, 640, 768
K_I48, K_A16, K_B16, K_P1, K_BD, K_DUM, K_T4 = 896, 944, 960, 976, 977, 985, 1001
K_MH = 1005
K_MT = 1009
NK = 1265


ONE = 1


def constants():
    k = np.zeros((P, NK), np.float32)
    p = np.arange(P)
    k[:, K_ID:K_ID + P] = np.eye(P)
    k[:, K_NEG + 384:K_NEG + 512] = np.where(p[None, :] > p[:, None], NEG, 0.0)
    k[:, K_U:K_U + P] = p[:, None] < p[None, :]
    k[:, K_ONE:K_ONE + P] = 1.0
    k[:, K_I48:K_I48 + NEW] = np.arange(NEW)
    k[:, K_A16:K_A16 + 16] = 16.0 * np.arange(16)
    k[:, K_B16:K_B16 + 16] = np.arange(16)
    k[:, K_P1] = p + 1
    k[:, K_BD:K_BD + 8] = p[:, None] // 16 == np.arange(8)[None, :]
    k[:, K_DUM:K_DUM + 16] = NTOK + 1 + (16 * (p[:, None] % 16) + np.arange(16)[None, :]) % HALF
    k[:, K_T4:K_T4 + TPC] = np.arange(TPC)
    k[:, K_MT:K_MT + P] = NEG
    k[:, K_MT + P:K_MT + 2 * P] = np.where(p[:, None] > p[None, :], NEG, 0.0)
    k[:, K_MH:K_MH + TPC] = -0.5
    return k


def rope_tables():
    d = np.arange(HD // 2, dtype=np.float32)
    theta = np.power(np.float32(10000.0), (-np.power(np.float32(2.0), d) / np.float32(HD)).astype(np.float32)).astype(np.float32)
    pos = np.arange(1, T + 1, dtype=np.float32)
    ang = (theta[:, None] * pos[None, :]).astype(np.float32)
    cos = np.cos(ang).astype(np.float32)
    sin = np.sin(ang).astype(np.float32)
    return (np.tile(np.concatenate([cos, cos]), (GH, 1)),
            np.tile(np.concatenate([-sin, sin]), (GH, 1)))


def plan():
    tiles = [(qb, c, min(CH, (qb + 1) * P - c * CH)) for qb in range(NT) for c in range(qb // TPC + 1)]
    units = []
    for j in range(NCH):
        units += [(j, kb, 0, False) for kb in range(0, TPC * j, 2)]
        units += [(j, TPC * j, 0, True), (j, TPC * j + 2, 2 * P, True)]
    return tiles, units


TILES, UNITS = plan()
NTILE, NU = len(TILES), len(UNITS)
NS2 = GH * NU
NPROJ = 3 * NCH
FIRST_USES = NPROJ + NTILE + 1
GROUP_USES = NPROJ + GH * (NTILE + 1)
BATCH_USES = FIRST_USES + (NG - 1) * GROUP_USES + (GH - 1) * (NTILE + 1)
NPR = 3
LOADED_AT = 2


def split_kind(u):
    return 0 if UNITS[u][3] else 1 + u % 2


def counted(n, kinds):
    return sum(split_kind(m % NU) in kinds for m in range(n))


def opening():
    out = []
    tiles = [("max", 0, i) for i in range(NTILE)]
    for j in range(NCH):
        values = j if j < 2 else j - 1
        out += [("proj", 2 * j), ("proj", 2 * j + 1), ("shuffle", j), ("turn", j, 0), ("turn", j, 1)]
        if j != 2:
            out.append(("vproj", values))
        out += [("sum", j), ("high", j), ("split", j)]
        if j != 2:
            out.append(("vsplit", values))
    return out + [("vproj", 3)] + tiles[:3] + [("vsplit", 3)] + tiles[3:] + [("row", 0)]


ROTATE = {"proj0": (-4, 2, 7, 12), "proj1": (-3, 4, 9, 14), "shuffle": (-3, 4, 9, 14), "turn0": (-2, 5, 10, 15),
          "turn1": (-1, 6, 11, 16), "sum": (1, 8, 13, 18), "high": (3, 8, 13, 18), "split": (4, 9, 14, 19)}
LAST_TILE = NU - 2


def reciprocals(j):
    return [("inverse", j, i) for i in range(TPC)] + [("scale", j)]


def attention(more):
    out, waiting, norms, inverses = [], [[], []], [], []
    beside = [[] for _ in range(GH * NU)]
    if more:
        for j in range(NCH):
            for what, steps in (("proj0", ("proj", 2 * j)), ("proj1", ("proj", 2 * j + 1)), ("shuffle", ("shuffle", j)),
                                ("turn0", ("turn", j, 0)), ("turn1", ("turn", j, 1)), ("sum", ("sum", j)),
                                ("high", ("high", j)), ("split", ("split", j))):
                beside[2 * NU + ROTATE[what][j]].append(steps)
    for h in range(GH):
        if more or h + 1 < GH:
            for i in range(NTILE):
                beside[NU * h + LOADED_AT + i * (LAST_TILE - LOADED_AT) // NTILE].append(("max", h + 1, i))
            beside[NU * h + LAST_TILE].append(("row", h + 1))
    for h in range(GH):
        for u in range(NU):
            out.append(("score", h, u))
            fill = beside[NU * h + u]
            half = (len(fill) + 1) // 2
            now = waiting.pop(0)
            first = [s for s in now if s[0] == "low" or s[0] == "value" and s[3]]
            rest = [s for s in now if s[0] == "value" and not s[3]]
            out += first + fill[:half] + rest[:1] + fill[half:] + rest[1:] + [s for s in now if s[0] == "copy"] + norms + inverses[:1]
            inverses = inverses[1:] + [s for n in norms if n[1] == GH - 1 for s in reciprocals(n[2])]
            norms = [s for s in now if s[0] == "norm"]
            if split_kind(u):
                waiting.append([("low", h, u), ("value", h, u, 1, 0), ("value", h, u, 1, 1), ("value", h, u, 0, 0), ("value", h, u, 0, 1)])
            else:
                waiting.append([("value", h, u, 0, 0), ("value", h, u, 0, 1)])
            if u == NU - 1 or UNITS[u + 1][0] != UNITS[u][0]:
                waiting[-1] += [("copy", h, UNITS[u][0]), ("norm", h, UNITS[u][0])]
    if more:
        out.append(("vproj", 0))
    out += norms + inverses + waiting[0] + waiting[1] + reciprocals(NCH - 1)
    if more:
        out += [("vsplit", 0)] + [(kind, j) for j in range(1, NCH) for kind in ("vproj", "vsplit")]
    return out


class Chain:

    def __init__(self, eng, sem, per):
        self.eng, self.sem, self.per = eng, sem, per

    def begin(self, n):
        self.base, self.k = n * self.per, 0

    def link(self, ins, passed=None):
        ins.then_inc(self.sem, 1)
        self.k += 1
        self.eng.wait_ge(self.sem, ONE + self.base + self.k)
        if passed is not None:
            self.eng.sem_inc(passed, 1)

    def end(self):
        assert self.k == self.per, self.k


def adaln_block(nc, x, wqkv, bqk, bv, wo, bo, cT, wmod, gwT, o2n_col, o2n_row, wgu, wdn, cos, sin, kst, out):
    with ExitStack() as ctx:
        sems = []

        def sem(name, bumped=True):
            s = ctx.enter_context(nc.semaphore(name))
            if bumped:
                sems.append(s)
            return s

        def dram(name, shape, dt=F32):
            return nc.dram_tensor(name, shape, dt, kind="Internal").ap()

        modd = dram("modd", [NB, 6 * C])
        gbd = dram("gbd", [NB + 1, C])
        otd = dram("otd", [NB, NG, P, T])
        table = dram("table", [NROW, ROW])
        idxd = dram("idxd", [2, NEW * 256], I32)

        at = [0]

        def place(name, shape, dt):
            size = int(np.prod(shape[1:])) * (2 if dt == BF16 else 4)
            t = nc.alloc_sbuf_tensor_at(name, shape, dt, offset=BASE + at[0])
            at[0] += (size + 63) // 64 * 64
            return t

        BASE = (nc.sbuf_base + 63) // 64 * 64

        K = place("consts", [P, NK], F32)
        hT = place("hT", [P, KT, T], F32)
        modc = place("modc", [P, NB, 2 * KT], F32)
        Ubf = place("Ubf", [P, P], BF16)
        onesbf = place("onesbf", [P, P], BF16)
        idbf = place("idbf", [P, P], BF16)
        mtbf = place("mtbf", [P, 2 * P], BF16)
        Mold = place("Mold", [P, NEW], F32)
        Mbf = place("Mbf", [P, NEW], BF16)
        negb = place("negb", [P, NOLD], F32)
        Racc = place("Racc", [P, 6, 256], F32)
        tot = place("tot", [P, NEW], F32)
        tcol = place("tcol", [P, TPC], F32)
        PHASE = at[0]

        csT = place("csT", [P, KT, NB], F32)
        ce = place("ce", [P, KT, NB], F32)
        wm = place("wm", [P, KT, 6 * C], F32)
        mods = place("mods", [NB, 6 * C], F32)
        sgn = place("sgn", [NB, C], F32)
        oc = place("oc", [P, 1], I32)
        ocf = place("ocf", [P, 1], F32)
        orow = place("orow", [P, NOLD], I32)
        zrow = place("zrow", [HALF, ROW], F32)

        at[0] = PHASE
        cs = place("cs", [P, 2, T], F32)
        W = place("W", [P, KT, 3 * P], F32)
        bqg = place("bqg", [P, 2], F32)
        bvg = place("bvg", [P, P], F32)
        AFTER_WEIGHTS = at[0]
        part = place("part", [P, NT, NCH], F32)
        mx = place("mx", [P, NT], F32)
        mT = place("mT", [NT, P], F32R)
        QK = place("QK", [P, 2, 2, T], F32R)
        st = place("st", [P, 4, T], F32R)
        V = place("V", [P, NT, 2, 5, HD], F32R)
        vraw = place("vraw", [P, TPC, GH, HD], F32)
        den = place("den", [P, T], F32)
        ot = place("ot", [P, T], F32)
        at_full = at[0]
        Pfull = place("Pfull", [P, NPR, 2, CH], F32)
        at[0] = at_full
        Plow = place("Plow", [P, NPR, 2, CH], F32R)
        Phigh = place("Phigh", [P, NPR, 2, CH], F32R)
        qraw = place("qraw", [P, 2, CH], F32)
        qs = place("qs", [P, 2, CH], F32)
        t1 = place("t1", [P, 2, CH], F32)

        at[0] = AFTER_WEIGHTS
        xin = place("xin", [P, 2, TPC, C], F32)
        xhat = place("xhat", [P, TPC, C], F32)
        stA = place("stA", [P, TPC, 6], F32)
        mvA = place("mvA", [P, TPC, 2], F32)
        rsA = place("rsA", [P, TPC], F32)

        at[0] = PHASE
        wot = place("wot", [P, KT, C], F32)
        gwt = place("gwt", [P, KT, NOLD], F32)
        rows = place("rows", [P, 5, C], F32)
        otc = place("otc", [P, KT, CH], F32)
        xc = place("xc", [P, TPC, C], F32)
        x1 = place("x1", [P, 2, TPC, C], F32)
        h2 = place("h2", [P, TPC, C], F32)
        h2T = place("h2T", [P, KT, CH], F32)
        stC = place("stC", [P, TPC, 6], F32)
        mvC = place("mvC", [P, TPC, 2], F32)
        rsC = place("rsC", [P, TPC], F32)
        key = place("key", [P, TPC, NOLD], F32)
        lmx = place("lmx", [P, TPC], F32)
        ex = place("ex", [P, TPC, NOLD], F32)
        top = place("top", [P, TPC, 8], F32)
        rep = place("rep", [P, TPC, NOLD], F32)
        msk = place("msk", [P, TPC, NOLD], F32)
        gs = place("gs", [P, TPC], F32)
        gT = place("gT", [P, TPC, P], F32)
        mTb = place("mTb", [P, TPC, P], BF16)
        gN = place("gN", [P, TPC, NEW], F32)
        mN = place("mN", [P, TPC, NEW], BF16)
        pos = place("pos", [P, TPC, NEW], F32)
        posi = place("posi", [P, TPC, NEW], I32)
        hi = place("hi", [P, TPC, NEW], I32)
        lo = place("lo", [P, TPC, NEW], I32)
        Aoh = place("Aoh", [P, TPC, NEW, 16], BF16)
        B1 = place("B1", [P, TPC, 6, P], BF16)
        B2 = place("B2", [P, TPC, 6, 2, P], BF16)

        at[0] = PHASE
        Rd = place("Rd", [P, 6, 2, 8, 16], F32)
        slot = place("slot", [P, 6, 2, 16], F32)
        tok1 = place("tok1", [P, 6, 16], F32)
        emp = place("emp", [P, 6, 16], F32)
        sidx = place("sidx", [P, 2, 6, 16], I32)
        it = place("it", [HALF, TURN, 2, 2], I32)
        X = place("X", [HALF, HELD, 2, ROW], F32)
        GBr = place("GBr", [HALF, HELD, 2, C], F32)
        Wg = place("Wg", [P, HELD, KT, 2 * INTER], F32)
        Wd = place("Wd", [HALF, HELD, 2, C], F32)
        XT = place("XT", [P, 2, 2, 2, CAP], F32)
        e1 = place("e1", [HALF, 2, 2, CAP], F32)
        hb = place("hb", [HALF, 2, 2, CAP], F32)
        wv = place("wv", [HALF, 2, 2], F32)
        z = place("z", [HALF, HELD, 2, C], F32)

        PS = ctx.enter_context(nc.psum_tensor("PS", [P, 8, 512], F32))
        S1 = [PS[:, 0], PS[:, 1]]
        S2 = [PS[:, 2:4], PS[:, 4:6]]
        O = [PS[:, 6], PS[:, 7]]

        ident = K[:, K_ID:K_ID + P]

        consts_in = sem("consts_in")
        passed = sem("passed")
        mod_in = sem("mod_in")
        prep = sem("prep")
        silu_e = sem("silu_e")
        cs_ready = sem("cs_ready")
        mod_ps = sem("mod_ps")
        mod_sb = sem("mod_sb")
        mod_done = sem("mod_done")
        modT_ps = sem("modT_ps")
        modT_sb = sem("modT_sb")
        mod_out = sem("mod_out")
        zero_ready = sem("zero_ready")
        phase = sem("phase")

        x_in = [sem("x_in0"), sem("x_in1")]
        xhat_ready = sem("xhat_ready")
        hT_ps = sem("hT_ps")
        hT_sb = sem("hT_sb")
        chA = sem("chA")
        var_ready = sem("var_ready")
        rs_done = sem("rs_done")
        varC_ready = sem("varC_ready")
        rsC_done = sem("rsC_done")

        w_in = sem("w_in")
        ones_set = sem("ones_set")
        q_shuf = sem("q_shuf")
        rope_mul = sem("rope_mul")
        rope_add = sem("rope_add")
        q_hi = sem("q_hi")
        q_lo = sem("q_lo")
        qk_in = [sem("qk_in0"), sem("qk_in1")]
        s1_ready = sem("s1_ready")
        s1_free = sem("s1_free")
        max_all = sem("max_all")
        mt_ready = sem("mt_ready")
        mrow_in = sem("mrow_in")
        s2_ready = sem("s2_ready")
        exp_done = sem("exp_done")
        full_done = sem("full_done")
        p_low = [sem("p_low0"), sem("p_low1")]
        v_hi = sem("v_hi")
        v_lo = sem("v_lo")
        o_den = sem("o_den")
        pv_done = sem("pv_done")
        o_rec = sem("o_rec")
        o_norm = sem("o_norm")
        den_inv = sem("den_inv")
        ot_ready = sem("ot_ready")
        ot_out = sem("ot_out")

        rows_in = sem("rows_in")
        y_in = sem("y_in")
        c_in = sem("c_in")
        gabo = sem("gabo")
        xg_ready = sem("xg_ready")
        y_ps = sem("y_ps")
        y_used = sem("y_used")
        x1_ready = sem("x1_ready")
        h2_ready = sem("h2_ready")
        x1_out = [sem("x1_out0"), sem("x1_out1")]
        h2_out = sem("h2_out")
        t_ps = sem("t_ps")
        t_sb = sem("t_sb")
        l_ps = sem("l_ps")
        key_ready = sem("key_ready")
        ex_ready = sem("ex_ready")
        g_ready = sem("g_ready")
        gt_ps = sem("gt_ps")
        gt_sb = sem("gt_sb")
        n_ps = sem("n_ps")
        n_sb = sem("n_sb")
        g_out = sem("g_out")
        p_ps = sem("p_ps")
        pos_ready = sem("pos_ready")
        ab_ready = sem("ab_ready")
        r_ps = sem("r_ps")
        r_sb = sem("r_sb")
        chX = sem("chX")
        chK = sem("chK")
        chP = sem("chP")

        chD = sem("chD")
        slots_sb = sem("slots_sb")
        slots_out = sem("slots_out")
        it_in = [sem("it_in%d" % i) for i in range(TURN)]
        we_in = [sem("we_in%d" % i) for i in range(HELD)]
        xg_in = [sem("xg_in%d" % i, False) for i in range(HELD)]
        xt_ps = sem("xt_ps")
        xt_sb = sem("xt_sb")
        gu_ps = sem("gu_ps")
        e_ready = sem("e_ready")
        chE = sem("chE")
        h_ready = sem("h_ready")
        d_ps = sem("d_ps")
        wv_ready = sem("wv_ready")
        z_ready = sem("z_ready")
        scat = sem("scat", False)
        landed = sem("landed")

        ENGINES = 5
        NS_FULL = counted(NS2, (1, 2))
        NS_SHARED = counted(NS2, (1,))
        LOADED = 6 * 16

        def later(ee, u, k):
            return (ee, u + k) if u + k < TURN else (ee + 1, u + k - TURN)

        def per_expert(eng, body):
            with eng.Fori(0, NEW // TURN - 1) as ee:
                for u in range(TURN):
                    body(ee, u, TURN)
            for u in range(TURN):
                body(NEW // TURN - 1, u, TURN - 1 - u)

        def gate_up_banks(u):
            b = 2 + 2 * (u % 2)
            return [PS[0:HALF, b + i, 0:2 * CAP].rearrange("p (k s) -> p k s", k=2) for i in range(2)]

        def wait_apart(eng, sem, value):
            eng.wait_ge(sem, value if sem in (scat, *xg_in) else ONE + value)
            eng.sem_inc(passed, 1)

        def meet(eng, n):
            eng.sem_inc(passed, 1)
            eng.drain().then_inc(phase, 1)
            wait_apart(eng, phase, ENGINES * n)

        def v_part(j, low):
            return V[:, TPC * j:TPC * (j + 1), :, low::3, :].rearrange("p t a b d -> p (t a) b d")

        def o_part(h, j, what):
            at = (what, (what + 1) % 3)[h % 2]
            return O[j % 2][at * HD:(at + 1) * HD, :]

        def low_part(eng, ops, gi, h, u, i):
            j, kb, q0, diag = UNITS[u]
            n = NU * h + u
            cols = slice(max(kb + i - TPC * j, 0) * P, CH)
            tiles = slice(i, i + 1)
            if split_kind(u) == 2:
                if i == 0:
                    return
                cols, tiles = slice(q0, CH), slice(0, 2)
            eng.wait_ge(full_done, ONE + NS_FULL * gi + counted(n + 1, (1, 2)))
            eng.wait_ge(exp_done, ONE + NS2 * gi + n + 1)
            ops.tensor_tensor(Plow[:, n % NPR, tiles, cols], Pfull[:, n % NPR, tiles, cols],
                              Phigh[:, n % NPR, tiles, cols].bitcast(F32), ALU.subtract).then_inc(p_low[i], 1)

        block = ctx.enter_context(nc.Block())

        @block.sync
        def _(sp):
            for s in sems:
                sp.sem_inc(s, HELD if s is landed else ONE)
            for dst, src in ((K[:, :], kst), (csT[:, :, :], cT), (wm[:, :, :], wmod),
                             (oc[:, :], o2n_col), (orow[:, :], o2n_row.partition_broadcast(P))):
                sp.dma_start(dst, src).then_inc(consts_in, 16)
            wait_apart(sp, mod_done, 1)
            wait_apart(sp, zero_ready, 1)
            sp.dma_start(modd, mods[:, :]).then_inc(mod_out, 16)
            sp.dma_start(gbd[0:NB, :], mods[:, GB * C:(GB + 1) * C]).then_inc(mod_out, 16)
            sp.dma_start(gbd[NB:NB + 1, :], zrow[0:1, 0:C]).then_inc(mod_out, 16)
            sp.dma_start(table[NTOK:NROW, :], zrow[:, :]).then_inc(mod_out, 16)
            sp.dma_start(out[NTOK:NROW, :], zrow[:, 0:C]).then_inc(mod_out, 16)
            wait_apart(sp, mod_out, 80)

            with sp.Fori(0, NB) as b:
                meet(sp, 3 * b + 1)
                with sp.Fori(0, NCH // 2) as jj:
                    for u in range(2):
                        wait_apart(sp, xhat_ready, TPC * (NCH * b + 2 * jj))
                        sp.dma_start(xin[:, u], x[b, 2 * jj + u].rearrange("(t p) c -> p t c", p=P)).then_inc(x_in[u], 16)
                sp.dma_start(cs[:, 0], cos).then_inc(w_in, 16)
                sp.dma_start(cs[:, 1], sin).then_inc(w_in, 16)
                def weights(g):
                    sp.dma_start(W[:, :, :], wqkv[g]).then_inc(w_in, 16)
                    sp.dma_start(bqg[:, :], bqk[g]).then_inc(w_in, 16)
                    sp.dma_start(bvg[:, :], bv[g].partition_broadcast(P)).then_inc(w_in, 16)

                weights(0)
                meet(sp, 3 * b + 2)
                def stacks(gi, h):
                    own = slice(h % GH * HD, (h % GH + 1) * HD)
                    for blk, pair in enumerate((st[own, 0::2], st[own, 1:3], st[own, 0::3])):
                        sp.dma_start(QK[blk * HD:(blk + 1) * HD, h % 2].bitcast(F32), pair.bitcast(F32)).then_inc(qk_in[h % 2], 16)

                def max_row(gi, h):
                    wait_apart(sp, mt_ready, GH * gi + h + 1)
                    sp.dma_start(QK[3 * HD:3 * HD + 1, h % 2, 0, :].bitcast(F32), mT[:, :].bitcast(F32)).then_inc(mrow_in, 16)

                def output_weights():
                    sp.dma_start(wot[:, :, :], wo).then_inc(rows_in, 16)
                    sp.dma_start(gwt[:, :, :], gwT).then_inc(rows_in, 16)
                    sp.dma_start(rows[:, 4], bo.partition_broadcast(P)).then_inc(rows_in, 16)
                    for i, m in ((0, GA), (2, CB1), (3, SB)):
                        sp.dma_start(rows[:, i], modd[b, m * C:(m + 1) * C].partition_broadcast(P)).then_inc(rows_in, 16)

                def group(b, g, more):
                    gi = NG * b + g
                    wait_apart(sp, s2_ready, NS2 * gi)
                    stacks(gi, 1)
                    wait_apart(sp, s1_free, BATCH_USES * b + GROUP_USES * g + FIRST_USES)
                    if more:
                        weights(g + 1)
                    else:
                        output_weights()
                    max_row(gi, 1)
                    for h in range(2, GH + more):
                        wait_apart(sp, s2_ready, NS2 * gi + NU * (h - 1))
                        if h == GH:
                            wait_apart(sp, q_lo, NCH * (gi + 2))
                        stacks(gi, h)
                        max_row(gi, h)
                    for j in range(NCH):
                        wait_apart(sp, ot_ready, NCH * gi + j + 1)
                        cols = slice(j * CH, (j + 1) * CH)
                        sp.dma_start(otd[b, g, :, cols], ot[:, cols]).then_inc(ot_out, 16)

                wait_apart(sp, q_lo, NCH * (NG * b + 1))
                stacks(NG * b, 0)
                max_row(NG * b, 0)
                with sp.Fori(0, NG - 1) as g:
                    group(b, g, True)
                group(b, NG - 1, False)
                wait_apart(sp, ot_out, 16 * NCH * NG * (b + 1))
                meet(sp, 3 * b + 3)
                def load_attention(j):
                    wait_apart(sp, y_ps, TPC * (NCH * b + j))
                    for g in range(NG):
                        sp.dma_start(otc[:, g], otd[b, g, :, j * CH:(j + 1) * CH]).then_inc(y_in, 16)

                def load_tokens(j):
                    wait_apart(sp, x1_ready, NCH * b + j)
                    sp.dma_start(xc[:, :, :], x[b, j].rearrange("(t p) c -> p t c", p=P)).then_inc(c_in, 16)

                def store_rows(j):
                    ci = NCH * b + j
                    wait_apart(sp, x1_ready, ci + 1)
                    sp.dma_start(out[bass.ds(ci * CH, CH), :].rearrange("(t p) c -> p t c", p=P), x1[:, j % 2]).then_inc(x1_out[j % 2], 16)
                    wait_apart(sp, h2_ready, ci + 1)
                    sp.dma_start(table[bass.ds(ci * CH, CH), 0:C].rearrange("(t p) c -> p t c", p=P), h2[:, :, :]).then_inc(h2_out, 16)

                load_attention(0)
                load_tokens(0)
                load_attention(1)
                load_tokens(1)
                store_rows(0)
                for j in range(NCH):
                    ci = NCH * b + j
                    if j + 2 < NCH:
                        load_attention(j + 2)
                    wait_apart(sp, n_sb, ci + 1)
                    sp.dma_start(table[bass.ds(ci * CH, CH), C:ROW].rearrange("(t p) c -> p t c", p=P), gN[:, :, :]).then_inc(g_out, 16)
                    if j + 2 < NCH:
                        load_tokens(j + 2)
                    if j + 1 < NCH:
                        store_rows(j + 1)
                for i in range(2):
                    wait_apart(sp, x1_out[i], 32 * (b + 1))
                wait_apart(sp, h2_out, 64 * (b + 1))
                wait_apart(sp, g_out, 64 * (b + 1))
            meet(sp, 3 * NB + 1)
            wait_apart(sp, slots_sb, 1)
            for i in range(2):
                sp.dma_start(idxd[i].rearrange("(g p b) -> p g b", g=6, p=P), sidx[:, i]).then_inc(slots_out, 16)
            wait_apart(sp, slots_out, 32)

            def weights_of(ee, u):
                sp.dma_start(Wg[:, u % HELD], wgu[TURN * ee + u]).then_inc(we_in[u % HELD], 16)
                sp.dma_start(Wd[:, u % HELD], wdn[TURN * ee + u]).then_inc(we_in[u % HELD], 16)

            for u in range(HELD):
                for i in range(2):
                    sp.dma_start(it[:, u, i, :], idxd[i, u * 256:u * 256 + CAP].rearrange("(f p) -> p f", p=HALF),
                                 allow_slow_non_contiguous=True).then_inc(it_in[u], 16)
            for u in range(HELD - 1):
                weights_of(0, u)

            def ahead_of(ee, u, follow):
                if follow >= HELD - 1:
                    wait_apart(sp, d_ps, 2 * (TURN * ee + u))
                    weights_of(*later(ee, u, HELD - 1))
                if follow >= HELD:
                    wait_apart(sp, landed, TURN * ee + u)
                    ee, u = later(ee, u, HELD)
                    for i in range(2):
                        sp.dma_start(it[:, u, i, :],
                                     idxd[i, bass.ds(ee * (256 * TURN) + u * 256, CAP)].rearrange("(f p) -> p f", p=HALF),
                                     allow_slow_non_contiguous=True).then_inc(it_in[u], 16)

            per_expert(sp, ahead_of)

        @block.gpsimd
        def _(pool):
            nc.gpsimd.memset(zrow[:, :], 0.0).then_inc(zero_ready, 1)
            nc.gpsimd.memset(tot[:, :], 0.0)
            nc.gpsimd.memset(Racc[:, :, :], 0.0)
            with pool.Fori(0, NB) as b:
                meet(pool, 3 * b + 1)
                with pool.Fori(0, NCH) as j:
                    wait_apart(pool, var_ready, NCH * b + j + 1)
                    nc.gpsimd.tensor_tensor(rsA[:, :], rsA[:, :], K[:, K_MH:K_MH + TPC], ALU.pow).then_inc(rs_done, 1)
                meet(pool, 3 * b + 2)
                nc.gpsimd.memset(QK[3 * HD:3 * HD + 1, :, 1, :].bitcast(F32), 1.0).then_inc(ones_set, 1)
                wait_apart(pool, ones_set, 3 * b + 1)
                nc.gpsimd.memset(part[:, :, :], -3e38).then_inc(ones_set, 1)
                nc.gpsimd.memset(V[:, :, :, 2, :].bitcast(F32), 1.0).then_inc(ones_set, 1)
                def run(gi, steps, rotated):
                    for step in steps:
                        if step[0] == "turn":
                            j, i = step[1:]
                            ck = NCH * gi + NCH * rotated + j
                            cols = slice(j * CH, (j + 1) * CH)
                            table_of = cs[:, i:i + 1, cols].broadcast_to([P, 2, CH])
                            pool.wait_ge(q_shuf, ONE + ck + 1)
                            if i == 0:
                                pool.wait_ge(q_lo, ONE + ck)
                                nc.gpsimd.tensor_tensor(t1[:, :, :], qraw[:, :, :], table_of, ALU.mult).then_inc(rope_mul, 1)
                            else:
                                nc.gpsimd.tensor_tensor(qs[:, :, :], qs[:, :, :], table_of, ALU.mult).then_inc(rope_mul, 1)
                        elif step[0] == "low":
                            low_part(pool, nc.gpsimd, gi, *step[1:], 1)
                        elif step[0] == "scale":
                            j = step[1]
                            cols = slice(j * CH, (j + 1) * CH)
                            pool.wait_ge(o_norm, ONE + NCH * GH * gi + NCH * (GH - 1) + j + 1)
                            pool.wait_ge(den_inv, ONE + TPC * NCH * gi + TPC * (j + 1))
                            nc.gpsimd.tensor_tensor(ot[:, cols], ot[:, cols], den[:, cols], ALU.mult).then_inc(ot_ready, 1)

                run(NG * b, opening(), 0)
                with pool.Fori(0, NG - 1) as g:
                    run(NG * b + g, attention(True), 1)
                run(NG * b + NG - 1, attention(False), 1)
                meet(pool, 3 * b + 3)
                pool.wait_ge(rows_in, ONE + 96 * (b + 1))
                nc.gpsimd.tensor_tensor(rows[:, 1], rows[:, 0], rows[:, 4], ALU.mult).then_inc(gabo, 1)
                wait_apart(pool, gabo, b + 1)
                with pool.Fori(0, NCH) as j:
                    ci = NCH * b + j
                    pool.wait_ge(c_in, ONE + 16 * (ci + 1))
                    nc.gpsimd.tensor_tensor(xc[:, :, :], xc[:, :, :], rows[:, 1:2].broadcast_to([P, TPC, C]), ALU.add).then_inc(xg_ready, 1)
                    wait_apart(pool, varC_ready, ci + 1)
                    nc.gpsimd.tensor_tensor(rsC[:, :], rsC[:, :], K[:, K_MH:K_MH + TPC], ALU.pow).then_inc(rsC_done, 1)
            meet(pool, 3 * NB + 1)

            def gather(ee, u):
                wait_apart(pool, it_in[u], 32 * (ee + 1))
                k = u % HELD
                for f in range(2):
                    pool.indirect_dma_start(X[:, k, f, :], None, table[:, :],
                                            bass.IndirectOffsetOnAxis(ap=it[:, u, 0, f:f + 1], axis=0)).then_inc(xg_in[k], 16)
                    pool.indirect_dma_start(GBr[:, k, f, :], None, gbd[:, :],
                                            bass.IndirectOffsetOnAxis(ap=it[:, u, 1, f:f + 1], axis=0)).then_inc(xg_in[k], 16)

            def scatter(ee, u, f):
                wait_apart(pool, z_ready, 2 * (TURN * ee + u) + f + 1)
                pool.indirect_dma_start(out[:, :], bass.IndirectOffsetOnAxis(ap=it[:, u, 0, f:f + 1], axis=0),
                                        z[:, u % HELD, f, :], None, compute_op=ALU.add).then_inc(scat, 16)

            def serve(ee, u, follow):
                wait_apart(pool, scat, 32 * TURN * ee + 32 * u + 16)
                scatter(ee, u, 1)
                if follow >= HELD:
                    gather(*later(ee, u, HELD))
                wait_apart(pool, scat, 32 * TURN * ee + 32 * u + 32)
                pool.sem_inc(landed, 1)
                if follow >= 1:
                    scatter(*later(ee, u, 1), 0)

            for u in range(HELD):
                gather(0, u)
            scatter(0, 0, 0)
            per_expert(pool, serve)
            pool.wait_ge(scat, 32 * NEW)

        @block.scalar
        def _(act):
            act.wait_ge(consts_in, ONE + 80)
            nc.scalar.activation(ce[:, :, :], csT[:, :, :], ACT.Exp, scale=-1.0).then_inc(silu_e, 1)
            with act.Fori(0, NB) as b:
                meet(act, 3 * b + 1)
                with act.Fori(0, NCH) as j:
                    ci = NCH * b + j
                    act.wait_ge(hT_ps, ONE + ci + 1)
                    for ct in range(KT):
                        nc.scalar.activation(hT[:, ct, bass.ds(j * CH, CH)], PS[:, ct], ACT.Identity,
                                             bias=modc[:, b, ct:ct + 1], scale=modc[:, b, KT + ct:KT + ct + 1]).then_inc(hT_sb, 1)
                meet(act, 3 * b + 2)
                def run(gi, s1, first, steps, ahead):
                    n1 = first
                    for step in steps:
                        n1 += step[0] in ("proj", "vproj", "max", "row")
                        if step[0] == "high":
                            j = step[1]
                            cols = slice(j * CH, (j + 1) * CH)
                            act.wait_ge(rope_add, ONE + NCH * gi + NCH * ahead + j + 1)
                            if j == 0:
                                for i in range(2):
                                    act.wait_ge(qk_in[i], ONE + 96 * gi + 96 * ahead)
                            nc.scalar.activation(st[:, 0::2, cols], t1[:, :, :], ACT.Copy).then_inc(q_hi, 1)
                        elif step[0] == "vsplit":
                            j = step[1]
                            act.wait_ge(s1_free, ONE + s1 + n1)
                            if j == 0:
                                act.wait_ge(pv_done, ONE + NS2 * gi + NS2 * ahead)
                            nc.scalar.activation(v_part(j, 0), vraw[:, :, :, :].rearrange("p t (a b) d -> p (t a) b d", a=2), ACT.Copy).then_inc(v_hi, 1)
                        elif step[0] == "copy":
                            h, j = step[1:]
                            last_u = max(u for u in range(NU) if UNITS[u][0] == j)
                            act.wait_ge(pv_done, ONE + NS2 * gi + NU * h + last_u + 1)
                            if h == 0 and j == 0:
                                act.wait_ge(ot_out, ONE + 16 * NCH * gi)
                            own, cols = slice(h * HD, (h + 1) * HD), slice(j * CH, (j + 1) * CH)
                            nc.scalar.activation(ot[own, cols], o_part(h, j, 0), ACT.Copy).then_inc(o_rec, 1)
                            nc.scalar.activation(den[own, cols], o_part(h, j, 2), ACT.Copy).then_inc(o_den, 1)
                        elif step[0] == "score":
                            h, u = step[1:]
                            j, kb, q0, diag = UNITS[u]
                            n = NU * h + u
                            act.wait_ge(s2_ready, ONE + NS2 * gi + n + 1)
                            act.wait_ge(pv_done, ONE + NS2 * gi + max(n + 1 - NPR, 0))
                            cols = slice(q0, CH)
                            split = split_kind(u) > 0
                            nc.scalar.activation(Pfull[:, n % NPR, :, cols], S2[n % 2][:, :, cols], ACT.Exp,
                                                 scale=SCALE).then_inc(full_done if split else exp_done, 1)
                            if split:
                                nc.scalar.activation(Phigh[:, n % NPR, :, cols], S2[n % 2][:, :, cols], ACT.Exp, scale=SCALE).then_inc(exp_done, 1)

                run(NG * b, BATCH_USES * b, 0, opening(), 0)
                with act.Fori(0, NG - 1) as g:
                    run(NG * b + g, BATCH_USES * b + GROUP_USES * g, FIRST_USES, attention(True), 1)
                run(NG * b + NG - 1, BATCH_USES * b, GROUP_USES * (NG - 1) + FIRST_USES, attention(False), 1)
                meet(act, 3 * b + 3)

                def turned(j):
                    for t in range(TPC):
                        act.wait_ge(t_ps, ONE + TPC * (NCH * b + j) + t + 1)
                        nc.scalar.activation(h2T[:, :, t * P:(t + 1) * P], PS[:, 2].rearrange("p (c q) -> p c q", c=KT), ACT.Copy).then_inc(t_sb, 1)

                turned(0)
                for j in range(NCH):
                    ci = NCH * b + j
                    act.wait_ge(key_ready, ONE + ci + 1)
                    nc.scalar.activation(ex[:, :, :], key[:, :, :], ACT.Exp).then_inc(ex_ready, 1)
                    act.wait_ge(gt_ps, ONE + 2 * ci + 1)
                    nc.scalar.activation(gT[:, :, :], PS[:, 2].rearrange("p (c q) -> p c q", c=TPC), ACT.Copy).then_inc(gt_sb, 1)
                    act.wait_ge(gt_ps, ONE + 2 * ci + 2)
                    nc.scalar.activation(mTb[:, :, :], PS[:, 2].rearrange("p (c q) -> p c q", c=TPC), ACT.Copy).then_inc(gt_sb, 1)
                    if j + 1 < NCH:
                        turned(j + 1)
            meet(act, 3 * NB + 1)

            def xt_copy(ee, u):
                e = TURN * ee + u
                for i in range(2):
                    act.wait_ge(xt_ps, ONE + 2 * e + i + 1)
                    nc.scalar.activation(XT[:, u % 2, i], PS[:, i, 0:2 * CAP].rearrange("p (k s) -> p k s", k=2), ACT.Copy).then_inc(xt_sb, 1)

            def exp_gate(ee, u):
                e = TURN * ee + u
                act.wait_ge(gu_ps, ONE + 2 * e + 1)
                act.wait_ge(h_ready, ONE + e)
                nc.scalar.activation(e1[:, u % 2], gate_up_banks(u)[0], ACT.Exp, scale=-1.0).then_inc(e_ready, 1)

            def expert(ee, u, follow):
                if follow >= 1:
                    exp_gate(*later(ee, u, 1))
                if follow >= 2:
                    xt_copy(*later(ee, u, 2))

            xt_copy(0, 0)
            exp_gate(0, 0)
            xt_copy(0, 1)
            per_expert(act, expert)

        @block.tensor
        def _(pe):
            mm = nc.tensor.matmul
            pe.wait_ge(cs_ready, ONE + 1)
            for m in range(6):
                for k in range(KT):
                    last = mm(PS[0:NB, m], csT[:, k, :], wm[:, k, m * C:(m + 1) * C], start=k == 0, stop=k == KT - 1)
                last.then_inc(mod_ps, 1)
            pe.wait_ge(mod_done, ONE + 1)
            for i in range(2 * KT):
                m, ct = (SA, i) if i < KT else (CA1, i - KT)
                last = nc.tensor.transpose(PS[:, 6, i * NB:(i + 1) * NB], mods[:, m * C + ct * P:m * C + (ct + 1) * P], K[0:NB, K_ID:K_ID + NB])
            last.then_inc(modT_ps, 1)

            with pe.Fori(0, NB) as b:
                meet(pe, 3 * b + 1)
                with pe.Fori(0, NCH) as j:
                    ci = NCH * b + j
                    pe.wait_ge(hT_sb, ONE + KT * ci)
                    for t in range(TPC):
                        pe.wait_ge(xhat_ready, ONE + TPC * ci + t + 1)
                        for ct in range(KT):
                            last = nc.tensor.transpose(PS[:, ct, t * P:(t + 1) * P], xhat[:, t, ct * P:(ct + 1) * P], ident)
                    last.then_inc(hT_ps, 1)
                meet(pe, 3 * b + 2)
                def run(b, gi, s1, first, steps, ahead):
                    n1 = first
                    for step in steps:
                        kind, h = step[:2]
                        if kind in ("proj", "vproj", "max", "row"):
                            if kind == "proj" and h == 0:
                                pe.wait_ge(w_in, ONE + 32 * (b + 1) + 48 * (gi + 1 + ahead))
                            if kind == "max" and step[2] == 0:
                                pe.wait_ge(qk_in[h % 2], ONE + 96 * gi + 48 * (h // 2 + 1))
                            if kind == "row":
                                pe.wait_ge(max_all, ONE + GH * gi + h + 1)
                            pe.wait_ge(s1_free, ONE + s1 + max(n1 - 1, 0))
                        if kind == "proj":
                            j, i = h // 2, h % 2
                            for k in range(KT):
                                last = mm(S1[n1 % 2], W[:, k, i * P:(i + 1) * P], hT[:, k, j * CH:(j + 1) * CH], start=k == 0, stop=k == KT - 1)
                            last.then_inc(s1_ready, 1)
                            n1 += 1
                        elif kind == "vproj":
                            for t in range(TPC):
                                for k in range(KT):
                                    last = mm(S1[n1 % 2][:, t * P:(t + 1) * P], hT[:, k, h * CH + t * P:h * CH + (t + 1) * P],
                                              W[:, k, 2 * P:3 * P], start=k == 0, stop=k == KT - 1)
                            last.then_inc(s1_ready, 1)
                            n1 += 1
                        elif kind == "max":
                            qb, c, w = TILES[step[2]]
                            mm(S1[n1 % 2][:, 0:w], QK[0:3 * HD, h % 2, 0, qb * P:(qb + 1) * P], QK[0:3 * HD, h % 2, 1, c * CH:c * CH + w],
                               start=True, stop=True).then_inc(s1_ready, 1)
                            n1 += 1
                        elif kind == "row":
                            nc.tensor.transpose(S1[n1 % 2][0:NT, 0:P], mx[:, :], ident).then_inc(s1_ready, 1)
                            n1 += 1
                        elif kind == "score":
                            u = step[2]
                            j, kb, q0, diag = UNITS[u]
                            n = NU * h + u
                            if u == 0:
                                pe.wait_ge(mrow_in, ONE + 16 * (GH * gi + h + 1))
                            pe.wait_ge(exp_done, ONE + NS2 * gi + max(n - 1, 0))
                            for i in range(2):
                                last = mm(S2[n % 2][:, i, q0:CH], QK[0:3 * HD + 1, h % 2, 1, (kb + i) * P:(kb + i + 1) * P],
                                          QK[0:3 * HD + 1, h % 2, 0, j * CH + q0:(j + 1) * CH], start=True, stop=not diag)
                                if diag:
                                    last = mm(S2[n % 2][:, i, q0:q0 + (i + 1) * P], idbf[:, :], mtbf[:, (1 - i) * P:2 * P], start=False, stop=True)
                            last.then_inc(s2_ready, 1)
                        elif kind == "value":
                            u, high, i = step[2:]
                            j, kb, q0, diag = UNITS[u]
                            n = NU * h + u
                            r = max(kb + i - TPC * j, 0)
                            split = split_kind(u)
                            if i == 0 and (high or not split):
                                pe.wait_ge(exp_done, ONE + NS2 * gi + n + 1)
                                if n == 0:
                                    pe.wait_ge(v_lo, ONE + NCH * (gi + 1))
                                if kb == 0:
                                    pe.wait_ge(o_den, ONE + NCH * GH * gi + max(NCH * h + j - 1, 0))
                                    pe.wait_ge(o_norm, ONE + NCH * GH * gi + max(NCH * h + j - 1, 0))
                            if split == 1 and not high and i == 0:
                                pe.wait_ge(p_low[0], ONE + NS_SHARED * gi + counted(n + 1, (1,)))
                            elif split and not high:
                                pe.wait_ge(p_low[1], ONE + NS_FULL * gi + counted(n + 1, (1, 2)))
                            v_of = V[:, kb + i, h // 2].rearrange("p a d -> p (a d)")[:, 2 * HD * (h % 2):2 * HD * (h % 2) + 3 * HD]
                            p_of = (Phigh if high else Plow if split else Pfull)[:, n % NPR, i, r * P:CH]
                            if not split:
                                v_of = v_of.bitcast(F32)
                            last = mm(O[j % 2][0:3 * HD, r * P:CH], v_of, p_of,
                                      start=kb + i == 0 and (high == 1 or not split), stop=kb + i == TPC * (j + 1) - 1 and high == 0)
                            if i == 1 and not high:
                                last.then_inc(pv_done, 1)

                run(b, NG * b, BATCH_USES * b, 0, opening(), 0)
                wait_apart(pe, ones_set, 3 * (b + 1))
                with pe.Fori(0, NG - 1) as g:
                    run(b, NG * b + g, BATCH_USES * b + GROUP_USES * g, FIRST_USES, attention(True), 1)
                run(b, NG * b + NG - 1, BATCH_USES * b, GROUP_USES * (NG - 1) + FIRST_USES, attention(False), 1)
                meet(pe, 3 * b + 3)
                wait_apart(pe, rows_in, 96 * (b + 1))

                def output(j, tiles):
                    ci = NCH * b + j
                    if 0 in tiles:
                        pe.wait_ge(y_in, ONE + 64 * (ci + 1))
                    for t in tiles:
                        pe.wait_ge(y_used, ONE + TPC * NCH * b + max(TPC * j + t - 1, 0))
                        for k in range(KT):
                            last = mm(PS[:, t % 2], otc[:, k, t * P:(t + 1) * P], wot[:, k, :], start=k == 0, stop=k == KT - 1)
                        last.then_inc(y_ps, 1)

                def router(j):
                    ci = NCH * b + j
                    pe.wait_ge(h2_ready, ONE + ci + 1)
                    for t in range(TPC):
                        if t == 0:
                            pe.wait_ge(gt_sb, ONE + 2 * ci)
                        pe.wait_ge(t_sb, ONE + TPC * ci + t)
                        for ct in range(KT):
                            last = nc.tensor.transpose(PS[:, 2, ct * P:(ct + 1) * P], h2[:, t, ct * P:(ct + 1) * P], ident)
                        last.then_inc(t_ps, 1)
                    pe.wait_ge(t_sb, ONE + TPC * (ci + 1))
                    pe.wait_ge(pos_ready, ONE + ci)
                    for t in range(TPC):
                        for ct in range(KT):
                            last = mm(PS[:, 3, t * NOLD:(t + 1) * NOLD], h2T[:, ct, t * P:(t + 1) * P], gwt[:, ct, :], start=ct == 0, stop=ct == KT - 1)
                    last.then_inc(l_ps, 1)

                def by_new_number(j):
                    ci = NCH * b + j
                    pe.wait_ge(g_ready, ONE + ci + 1)
                    for i, src in enumerate((ex, msk)):
                        pe.wait_ge(gt_sb, ONE + 2 * ci + i)
                        for t in range(TPC):
                            last = nc.tensor.transpose(PS[:, 2, t * P:(t + 1) * P], src[:, t, :], ident)
                        last.then_inc(gt_ps, 1)
                    pe.wait_ge(gt_sb, ONE + 2 * ci + 2)
                    pe.wait_ge(n_sb, ONE + ci)
                    for t in range(TPC):
                        mm(PS[:, 4, t * 96:t * 96 + NEW], gT[:, t, :], Mold[:, :], start=True, stop=True)
                        last = mm(PS[:, 4, t * 96 + NEW:t * 96 + 96], mTb[:, t, :], Mbf[:, :], start=True, stop=True)
                    last.then_inc(n_ps, 1)
                    pe.wait_ge(n_sb, ONE + ci + 1)
                    for t in range(TPC + 1):
                        o = PS[:, 3, t * NEW:(t + 1) * NEW]
                        for s in range(t):
                            last = mm(o, onesbf[:, :], mN[:, s, :], start=s == 0, stop=t == TPC and s == t - 1)
                        if t < TPC:
                            last = mm(o, Ubf[:, :], mN[:, t, :], start=t == 0, stop=True)
                    last.then_inc(p_ps, 1)

                def slots(j):
                    ci = NCH * b + j
                    pe.wait_ge(ab_ready, ONE + ci + 1)
                    pe.wait_ge(r_sb, ONE + ci)
                    for g in range(6):
                        for t in range(TPC):
                            last = mm(PS[:, 5 + g // 2, (g % 2) * 256:(g % 2 + 1) * 256],
                                      Aoh[:, t, 8 * g:8 * g + 8, :].rearrange("p e a -> p (e a)"),
                                      B2[:, t, g].rearrange("p v c -> p (v c)"), start=t == 0, stop=t == TPC - 1)
                    last.then_inc(r_ps, 1)

                output(0, range(TPC))
                router(0)
                output(1, range(TPC))
                for j in range(NCH):
                    by_new_number(j)
                    if j + 2 < NCH:
                        output(j + 2, (0, 1))
                    if j + 1 < NCH:
                        router(j + 1)
                    if j + 2 < NCH:
                        output(j + 2, (2, 3))
                    slots(j)
            meet(pe, 3 * NB + 1)

            def turn(ee, u):
                e = TURN * ee + u
                pe.wait_ge(xg_in[u % HELD], 64 * (TURN // HELD * ee + u // HELD + 1))
                pe.wait_ge(xt_sb, ONE + 2 * e)
                for i in range(2):
                    for kk in range(2):
                        for f in range(2):
                            ct = 2 * i + kk
                            last = nc.tensor.transpose(PS[:, i, kk * CAP + f * HALF:kk * CAP + (f + 1) * HALF],
                                                       X[:, u % HELD, f, ct * P:(ct + 1) * P], K[0:HALF, K_ID:K_ID + HALF])
                    last.then_inc(xt_ps, 1)

            def gate_up(ee, u):
                e = TURN * ee + u
                pe.wait_ge(xt_sb, ONE + 2 * e + 2)
                pe.wait_ge(we_in[u % HELD], ONE + 32 * (TURN // HELD * ee + u // HELD + 1))
                banks = gate_up_banks(u)
                for i in range(2):
                    for q in range(2):
                        for k in range(KT):
                            o = (2 * i + q) * HALF
                            last = mm(banks[i][:, q, :], Wg[:, u % HELD, k, o:o + HALF], XT[:, u % 2, k // 2, k % 2, :],
                                      start=k == 0, stop=k == KT - 1)
                    last.then_inc(gu_ps, 1)

            def down(ee, u):
                e = TURN * ee + u
                pe.wait_ge(h_ready, ONE + e + 1)
                pe.wait_ge(z_ready, ONE + 2 * e)
                for f in range(2):
                    for q in range(2):
                        last = mm(PS[0:HALF, 6 + f, :], hb[:, u % 2, q, f * HALF:(f + 1) * HALF], Wd[:, u % HELD, q, :], start=q == 0, stop=q == 1)
                    last.then_inc(d_ps, 1)

            def expert(ee, u, follow):
                if follow >= 1:
                    gate_up(*later(ee, u, 1))
                if follow >= 2:
                    turn(*later(ee, u, 2))
                down(ee, u)

            turn(0, 0)
            gate_up(0, 0)
            turn(0, 1)
            per_expert(pe, expert)

        @block.vector
        def _(dve):
            v = nc.vector
            pre = Chain(dve, prep, 20)
            pre.begin(0)
            dve.wait_ge(consts_in, ONE + 80)
            dve.wait_ge(silu_e, ONE + 1)
            pre.link(v.tensor_scalar(ce[:, :, :], ce[:, :, :], 1.0, None, ALU.add))
            pre.link(v.reciprocal(ce[:, :, :], ce[:, :, :]))
            v.tensor_tensor(csT[:, :, :], csT[:, :, :], ce[:, :, :], ALU.mult).then_inc(cs_ready, 1)
            v.tensor_copy(Ubf[:, :], K[:, K_U:K_U + P])
            v.tensor_copy(onesbf[:, :], K[:, K_ONE:K_ONE + P])
            v.tensor_copy(idbf[:, :], K[:, K_ID:K_ID + P])
            v.tensor_copy(mtbf[:, :], K[:, K_MT:K_MT + 2 * P])
            v.tensor_copy(tcol[:, :], K[:, K_T4:K_T4 + TPC])
            pre.link(v.tensor_copy(ocf[:, :], oc[:, :]))
            pre.link(v.tensor_scalar(Mold[:, :], K[:, K_I48:K_I48 + NEW], ocf[:, :], None, ALU.is_equal))
            v.tensor_copy(Mbf[:, :], Mold[:, :])
            pre.link(v.tensor_copy(negb[:, :], orow[:, :]))
            pre.link(v.tensor_scalar(negb[:, :], negb[:, :], -1.0, NEG, ALU.is_equal, ALU.mult))
            for m in range(6):
                dve.wait_ge(mod_ps, ONE + m + 1)
                dst = mods[:, m * C:(m + 1) * C]
                if m in (CA1, CB1):
                    pre.link(v.tensor_scalar(dst, PS[0:NB, m], 1.0, None, ALU.add))
                elif m in (GA, GB):
                    pre.link(v.tensor_scalar(sgn[:, :], PS[0:NB, m], 0.0, 2.0, ALU.is_ge, ALU.mult))
                    pre.link(v.tensor_scalar(sgn[:, :], sgn[:, :], 1.0, None, ALU.subtract))
                    pre.link(v.tensor_tensor(dst, PS[0:NB, m], sgn[:, :], ALU.mult))
                    pre.link(v.tensor_scalar(dst, dst, 0.25, None, ALU.max))
                    if m == GB:
                        v.tensor_tensor(dst, dst, sgn[:, :], ALU.mult).then_inc(mod_done, 1)
                    else:
                        pre.link(v.tensor_tensor(dst, dst, sgn[:, :], ALU.mult))
                else:
                    pre.link(v.tensor_copy(dst, PS[0:NB, m]))
            dve.wait_ge(modT_ps, ONE + 1)
            pre.link(v.tensor_copy(modc[:, :, :].rearrange("p b k -> p k b"), PS[:, 6, 0:2 * KT * NB].rearrange("p (k b) -> p k b", b=NB)))
            pre.end()

            a = Chain(dve, chA, 2)
            cx, ck, cp = Chain(dve, chX, 3), Chain(dve, chK, 9), Chain(dve, chP, 7)
            with dve.Fori(0, NB) as b:
                meet(dve, 3 * b + 1)
                with dve.Fori(0, NCH // 2) as jj:
                    for u in range(2):
                        ci = NCH * b + 2 * jj + u
                        a.begin(ci)
                        dve.wait_ge(x_in[u], ONE + 32 * b + 16 * jj + 16)
                        for t in range(TPC):
                            last = v.bn_stats(stA[:, t, :], xin[:, u, t, :])
                        a.link(last, passed)
                        for t in range(TPC):
                            last = v.bn_aggr(mvA[:, t, :], stA[:, t, :])
                        a.link(last)
                        v.tensor_scalar(rsA[:, :], mvA[:, :, 1], EPS, None, ALU.add).then_inc(var_ready, 1)
                        dve.wait_ge(rs_done, ONE + ci + 1)
                        dve.wait_ge(hT_ps, ONE + ci)
                        for t in range(TPC):
                            last = v.tensor_scalar(xhat[:, t, :], xin[:, u, t, :], mvA[:, t, 0:1], rsA[:, t:t + 1], ALU.subtract, ALU.mult)
                            last.then_inc(xhat_ready, 1)
                        a.end()
                meet(dve, 3 * b + 2)
                swap = list(range(HD // 2, HD)) + list(range(HD // 2))

                def run(gi, s1, first, steps, ahead):
                    n1 = first
                    for step in steps:
                        kind, h = step[:2]
                        if kind == "proj":
                            dve.wait_ge(s1_ready, ONE + s1 + n1 + 1)
                            dve.wait_ge(rope_mul, ONE + 2 * (NCH * gi + NCH * ahead + h // 2))
                            v.tensor_scalar(qraw[:, h % 2], S1[n1 % 2], bqg[:, h % 2:h % 2 + 1], None, ALU.add).then_inc(s1_free, 1)
                            n1 += 1
                        elif kind == "shuffle":
                            wait_apart(dve, s1_free, s1 + n1)
                            v.stream_shuffle(qs[:, :, :], qraw[:, :, :], swap).then_inc(q_shuf, 1)
                        elif kind == "sum":
                            ck = NCH * gi + NCH * ahead + h
                            dve.wait_ge(rope_mul, ONE + 2 * ck + 2)
                            v.tensor_tensor(t1[:, :, :], t1[:, :, :], qs[:, :, :], ALU.add).then_inc(rope_add, 1)
                        elif kind == "split":
                            ck = NCH * gi + NCH * ahead + h
                            cols = slice(h * CH, (h + 1) * CH)
                            dve.wait_ge(q_hi, ONE + ck + 1)
                            dve.wait_ge(rope_add, ONE + ck + 1)
                            v.tensor_tensor(st[:, 1::2, cols], t1[:, :, :], st[:, 0::2, cols], ALU.subtract).then_inc(q_lo, 1)
                        elif kind == "vproj":
                            dve.wait_ge(s1_ready, ONE + s1 + n1 + 1)
                            dve.wait_ge(v_lo, ONE + NCH * gi + NCH * ahead + h)
                            v.tensor_tensor(vraw[:, :, :, :], S1[n1 % 2].rearrange("p (t h d) -> p t h d", t=TPC, h=GH),
                                            bvg[:, :].rearrange("p (h d) -> p h d", h=GH).unsqueeze(1).broadcast_to([P, TPC, GH, HD]),
                                            ALU.add).then_inc(s1_free, 1)
                            n1 += 1
                        elif kind == "vsplit":
                            dve.wait_ge(v_hi, ONE + NCH * gi + NCH * ahead + h + 1)
                            v.tensor_tensor(v_part(h, 1), vraw[:, :, :, :].rearrange("p t (a b) d -> p (t a) b d", a=2),
                                            v_part(h, 0).bitcast(F32), ALU.subtract).then_inc(v_lo, 1)
                        elif kind == "low":
                            low_part(dve, v, gi, *step[1:], 0)
                        elif kind == "max":
                            qb, cc, w = TILES[step[2]]
                            if step[2] == 0 and not ahead:
                                wait_apart(dve, ones_set, 3 * (b + 1))
                            wait_apart(dve, s1_ready, s1 + n1 + 1)
                            if cc == qb // TPC:
                                v.tensor_tensor_reduce(out=S1[n1 % 2][:, 0:w], in0=S1[n1 % 2][:, 0:w], in1=K[:, K_NEG + CH - w:K_NEG + CH],
                                                       scale=1.0, scalar=-3e38, op0=ALU.add, op1=ALU.max,
                                                       accum_out=part[:, qb, cc:cc + 1]).then_inc(s1_free, 1)
                            else:
                                v.reduce_max(part[:, qb, cc:cc + 1], S1[n1 % 2][:, 0:w], AX.X).then_inc(s1_free, 1)
                            n1 += 1
                        elif kind == "row":
                            dve.wait_ge(s1_free, ONE + s1 + n1)
                            v.reduce_max(mx[:, :], part[:, :, :], AX.X).then_inc(max_all, 1)
                            dve.wait_ge(mrow_in, ONE + 16 * (GH * gi + h))
                            dve.wait_ge(s1_ready, ONE + s1 + n1 + 1)
                            v.tensor_scalar(mT[:, :], S1[n1 % 2][0:NT, 0:P], -1.0, None, ALU.mult).then_inc(mt_ready, 1)
                            dve.wait_ge(mt_ready, ONE + GH * gi + h + 1)
                            dve.sem_inc(s1_free, 1)
                            n1 += 1
                        elif kind == "norm":
                            j = step[2]
                            nn = NCH * h + j
                            last_u = max(u for u in range(NU) if UNITS[u][0] == j)
                            dve.wait_ge(pv_done, ONE + NS2 * gi + NU * h + last_u + 1)
                            own, cols = slice(h * HD, (h + 1) * HD), slice(j * CH, (j + 1) * CH)
                            dve.wait_ge(o_rec, ONE + NCH * GH * gi + nn + 1)
                            v.tensor_tensor(ot[own, cols], o_part(h, j, 1), ot[own, cols], ALU.add).then_inc(o_norm, 1)
                        elif kind == "inverse":
                            i = step[2]
                            cols = slice(h * CH + i * P, h * CH + (i + 1) * P)
                            dve.wait_ge(o_den, ONE + NCH * GH * gi + NCH * (GH - 1) + h + 1)
                            v.reciprocal(den[:, cols], den[:, cols]).then_inc(den_inv, 1)

                run(NG * b, BATCH_USES * b, 0, opening(), 0)
                with dve.Fori(0, NG - 1) as g:
                    run(NG * b + g, BATCH_USES * b + GROUP_USES * g, FIRST_USES, attention(True), 1)
                run(NG * b + NG - 1, BATCH_USES * b, GROUP_USES * (NG - 1) + FIRST_USES, attention(False), 1)
                meet(dve, 3 * b + 3)
                wait_apart(dve, rows_in, 96 * (b + 1))

                def gated(j, tiles):
                    ci = NCH * b + j
                    if 0 in tiles:
                        dve.wait_ge(x1_out[j % 2], ONE + 32 * b + 16 * (j // 2))
                    for t in tiles:
                        dve.wait_ge(y_ps, ONE + TPC * ci + t + 1)
                        v.tensor_tensor(x1[:, j % 2, t, :], PS[:, t % 2], rows[:, 0], ALU.mult).then_inc(y_used, 1)

                def normal(j):
                    ci = NCH * b + j
                    cx.begin(ci)
                    dve.wait_ge(y_used, ONE + TPC * (ci + 1))
                    dve.wait_ge(xg_ready, ONE + ci + 1)
                    v.tensor_tensor(x1[:, j % 2], x1[:, j % 2], xc[:, :, :], ALU.add).then_inc(x1_ready, 1)
                    dve.wait_ge(x1_ready, ONE + ci + 1)
                    for t in range(TPC):
                        last = v.bn_stats(stC[:, t, :], x1[:, j % 2, t, :])
                    cx.link(last, passed)
                    for t in range(TPC):
                        last = v.bn_aggr(mvC[:, t, :], stC[:, t, :])
                    cx.link(last)
                    v.tensor_scalar(rsC[:, :], mvC[:, :, 1], EPS, None, ALU.add).then_inc(varC_ready, 1)
                    dve.wait_ge(h2_out, ONE + 16 * ci)
                    for t in range(TPC):
                        last = v.scalar_tensor_tensor(h2[:, t, :], x1[:, j % 2, t, :], mvC[:, t, 0:1], rows[:, 2], ALU.subtract, ALU.mult)
                    cx.link(last)
                    dve.wait_ge(rsC_done, ONE + ci + 1)
                    for t in range(TPC):
                        last = v.scalar_tensor_tensor(h2[:, t, :], h2[:, t, :], rsC[:, t:t + 1], rows[:, 3], ALU.mult, ALU.add)
                    last.then_inc(h2_ready, 1)
                    cx.end()

                def gates(j):
                    ci = NCH * b + j
                    ck.begin(ci)
                    dve.wait_ge(l_ps, ONE + ci + 1)
                    ck.link(v.tensor_tensor(key[:, :, :], PS[:, 3].rearrange("p (t e) -> p t e", t=TPC),
                                           negb[:, :].unsqueeze(1).broadcast_to([P, TPC, NOLD]), ALU.add))
                    ck.link(v.reduce_max(lmx[:, :], key[:, :, :], AX.X))
                    v.tensor_tensor(key[:, :, :], key[:, :, :], lmx[:, :].unsqueeze(2).broadcast_to([P, TPC, NOLD]), ALU.subtract).then_inc(key_ready, 1)
                    dve.wait_ge(key_ready, ONE + ci + 1)
                    ck.link(v.tensor_scalar(rep[:, :, :], key[:, :, :], FLOOR, None, ALU.max), passed)
                    for t in range(TPC):
                        last = v.max(top[:, t, :], rep[:, t, :])
                    ck.link(last, passed)
                    for t in range(TPC):
                        last = v.match_replace(msk[:, t, :], top[:, t, :], rep[:, t, :], -3e38)
                    ck.link(last)
                    ck.link(v.tensor_scalar(msk[:, :, :], msk[:, :, :], -1e38, None, ALU.is_lt))
                    dve.wait_ge(ex_ready, ONE + ci + 1)
                    ck.link(v.tensor_tensor(ex[:, :, :], ex[:, :, :], msk[:, :, :], ALU.mult))
                    ck.link(v.reduce_sum(gs[:, :], ex[:, :, :], AX.X))
                    ck.link(v.reciprocal(gs[:, :], gs[:, :]))
                    v.tensor_tensor(ex[:, :, :], ex[:, :, :], gs[:, :].unsqueeze(2).broadcast_to([P, TPC, NOLD]), ALU.mult).then_inc(g_ready, 1)
                    ck.end()
                    dve.wait_ge(n_ps, ONE + ci + 1)
                    dve.wait_ge(g_out, ONE + 16 * ci)
                    pn = PS[:, 4, 0:TPC * 96].rearrange("p (t v e) -> p t v e", t=TPC, v=2)
                    v.tensor_copy(gN[:, :, :], pn[:, :, 0, :])
                    v.tensor_copy(mN[:, :, :], pn[:, :, 1, :]).then_inc(n_sb, 1)

                def positions(j):
                    ci = NCH * b + j
                    cp.begin(ci)
                    dve.wait_ge(p_ps, ONE + ci + 1)
                    dve.wait_ge(n_sb, ONE + ci + 1)
                    cp.link(v.tensor_tensor(pos[:, :, :], PS[:, 3, 0:TPC * NEW].rearrange("p (t e) -> p t e", t=TPC),
                                           tot[:, :].unsqueeze(1).broadcast_to([P, TPC, NEW]), ALU.add))
                    cp.link(v.tensor_tensor(tot[:, :], tot[:, :], PS[:, 3, TPC * NEW:(TPC + 1) * NEW], ALU.add))
                    cp.link(v.scalar_tensor_tensor(pos[:, :, :], mN[:, :, :], -BIG, pos[:, :, :], ALU.mult, ALU.add))
                    cp.link(v.tensor_scalar(posi[:, :, :], pos[:, :, :], BIG, None, ALU.add))
                    v.tensor_scalar(lo[:, :, :], posi[:, :, :], 15, None, ALU.bitwise_and).then_inc(pos_ready, 1)
                    cp.link(v.tensor_scalar(hi[:, :, :], posi[:, :, :], 0xFFFFF0, None, ALU.bitwise_and))
                    v.tensor_tensor(Aoh[:, :, :, :].rearrange("p t e a -> p (t e) a"),
                                    hi[:, :, :].rearrange("p t e -> p (t e)").unsqueeze(2).broadcast_to([P, TPC * NEW, 16]),
                                    K[:, K_A16:K_A16 + 16].unsqueeze(1).broadcast_to([P, TPC * NEW, 16]), ALU.is_equal)
                    dve.wait_ge(pos_ready, ONE + ci + 1)
                    cp.link(v.tensor_tensor(B1[:, :, :, :].rearrange("p t g (e b) -> p (t g e) b", b=16),
                                           lo[:, :, :].rearrange("p t e -> p (t e)").unsqueeze(2).broadcast_to([P, TPC * NEW, 16]),
                                           K[:, K_B16:K_B16 + 16].unsqueeze(1).broadcast_to([P, TPC * NEW, 16]), ALU.is_equal))
                    v.tensor_scalar(B2[:, :, :, 0, :].rearrange("p t g c -> p (t g) c"), B1[:, :, :, :].rearrange("p t g c -> p (t g) c"), K[:, K_P1:K_P1 + 1], None, ALU.mult)
                    for t in range(TPC):
                        last = v.tensor_scalar(B2[:, t, :, 1, :], B1[:, t, :, :], tcol[:, t:t + 1], None, ALU.mult)
                    last.then_inc(ab_ready, 1)
                    dve.wait_ge(ab_ready, ONE + ci + 1)
                    cp.link(v.tensor_scalar(tcol[:, :], tcol[:, :], float(TPC), None, ALU.add))
                    cp.end()

                gated(0, range(TPC))
                normal(0)
                gated(1, range(TPC))
                for j in range(NCH):
                    ci = NCH * b + j
                    gates(j)
                    if j + 1 < NCH:
                        normal(j + 1)
                    if j + 2 < NCH:
                        gated(j + 2, (0, 1))
                    positions(j)
                    if j + 2 < NCH:
                        gated(j + 2, (2, 3))
                    dve.wait_ge(r_ps, ONE + ci + 1)
                    v.tensor_tensor(Racc[:, :, :].rearrange("p (b g) c -> p b (g c)", g=2), Racc[:, :, :].rearrange("p (b g) c -> p b (g c)", g=2),
                                    PS[:, 5:8], ALU.add).then_inc(r_sb, 1)
                    dve.wait_ge(r_sb, ONE + ci + 1)
            meet(dve, 3 * NB + 1)
            d = Chain(dve, chD, 8)
            d.begin(0)
            d.link(v.tensor_tensor(Rd[:, :, :, :, :].rearrange("p g v e b -> p (g v) e b"),
                                   Racc[:, :, :].rearrange("p g (v e b) -> p (g v) e b", v=2, e=8),
                                   K[:, K_BD:K_BD + 8].unsqueeze(1).unsqueeze(3).broadcast_to([P, 12, 8, 16]), ALU.mult))
            d.link(v.reduce_sum(slot[:, :, :, :].rearrange("p g v b -> p (g v) b"),
                                Rd[:, :, :, :, :].rearrange("p g v e b -> p (g v) b e"), AX.X))
            d.link(v.scalar_tensor_tensor(tok1[:, :, :], slot[:, :, 1, :], float(P), slot[:, :, 0, :], ALU.mult, ALU.add))
            d.link(v.tensor_scalar(emp[:, :, :], tok1[:, :, :], 0.0, None, ALU.is_equal))
            d.link(v.tensor_tensor(emp[:, :, :], emp[:, :, :], K[:, K_DUM:K_DUM + 16].unsqueeze(1).broadcast_to([P, 6, 16]), ALU.mult))
            d.link(v.tensor_tensor(tok1[:, :, :], tok1[:, :, :], emp[:, :, :], ALU.add))
            d.link(v.tensor_scalar(sidx[:, 0], tok1[:, :, :], 1.0, None, ALU.subtract))
            d.link(v.tensor_scalar(sidx[:, 1], sidx[:, 0], 11, None, ALU.logical_shift_right))
            dve.sem_inc(slots_sb, 1)
            d.end()

            ch = Chain(dve, chE, 3)

            def hidden(ee, u):
                e = TURN * ee + u
                ch.begin(e)
                g2, u2 = gate_up_banks(u)
                t = e1[:, u % 2]
                dve.wait_ge(e_ready, ONE + e + 1)
                ch.link(v.tensor_scalar(t, t, 1.0, None, ALU.add))
                ch.link(v.reciprocal(t, t))
                ch.link(v.tensor_tensor(t, t, g2, ALU.mult))
                dve.wait_ge(gu_ps, ONE + 2 * e + 2)
                v.tensor_tensor(hb[:, u % 2], t, u2, ALU.mult).then_inc(h_ready, 1)
                ch.end()

            def scaled(ee, u):
                e = TURN * ee + u
                k = u % HELD
                dve.wait_ge(xg_in[k], 64 * (TURN // HELD * ee + u // HELD + 1))
                v.tensor_copy(wv[:, u % 2, :], X[:, k, :, bass.ds(C + TURN * ee + u, 1)].rearrange("p f o -> p (f o)")).then_inc(wv_ready, 1)
                dve.wait_ge(wv_ready, ONE + e + 1)
                dve.wait_ge(landed, ONE + e)
                for f in range(2):
                    dve.wait_ge(d_ps, ONE + 2 * e + f + 1)
                    v.scalar_tensor_tensor(z[:, k, f, :], PS[0:HALF, 6 + f, :], wv[:, u % 2, f:f + 1], GBr[:, k, f, :], ALU.mult, ALU.mult).then_inc(z_ready, 1)

            def expert(ee, u, follow):
                if follow >= 1:
                    hidden(*later(ee, u, 1))
                scaled(ee, u)

            hidden(0, 0)
            per_expert(dve, expert)


_INS = ("x", "wqkv", "bqk", "bv", "wo", "bo", "cT", "wmod", "gwT", "o2n_col", "o2n_row", "wgu", "wdn", "cos", "sin", "kst")


def laid_out(L0_attn_x, L0_attn_Wqkv, L0_attn_bqkv, L0_attn_Wo, L0_attn_bo, L0_ffn_gate_weight, L0_ffn_gate_up_proj,
             L0_ffn_down_proj, L0_ffn_old_to_new, L0_c, L0_wmod):
    def rows_first(w, n):
        return w.reshape(-1, P, n).transpose(1, 0, 2)

    w3 = np.asarray(L0_attn_Wqkv).reshape(3, NG, P, KT, P)
    b3 = np.asarray(L0_attn_bqkv).reshape(3, NG, P)
    cos, sin = rope_tables()
    gu = np.asarray(L0_ffn_gate_up_proj).transpose(0, 2, 1).reshape(NEW, KT, P, 2 * INTER)
    dn = np.asarray(L0_ffn_down_proj).transpose(0, 2, 1).reshape(NEW, 2, HALF, C)
    a = {
        "x": np.asarray(L0_attn_x).reshape(NB, NCH, CH, C),
        "wqkv": w3.transpose(1, 4, 3, 0, 2).reshape(NG, P, KT, 3 * P),
        "bqk": b3[:2].transpose(1, 2, 0),
        "bv": b3[2],
        "wo": rows_first(np.asarray(L0_attn_Wo).T, C),
        "bo": np.asarray(L0_attn_bo),
        "cT": rows_first(np.asarray(L0_c).T, NB),
        "wmod": rows_first(np.asarray(L0_wmod), 6 * C),
        "gwT": rows_first(np.asarray(L0_ffn_gate_weight).T, NOLD),
        "o2n_col": np.asarray(L0_ffn_old_to_new).reshape(NOLD, 1),
        "o2n_row": np.asarray(L0_ffn_old_to_new),
        "wgu": gu.transpose(0, 2, 1, 3),
        "wdn": dn.transpose(0, 2, 1, 3),
        "cos": cos, "sin": sin, "kst": constants(),
    }
    return {k: np.ascontiguousarray(v) for k, v in a.items()}


def kernel(**inputs):
    from concourse import bacc
    from concourse.bass_utils import run_bass_kernel_spmd

    nc = bacc.Bacc("TRN2", target_bir_lowering=False, num_devices=1)
    arrays = laid_out(**inputs)
    args = [nc.dram_tensor(n, arrays[n].shape, mybir.dt.from_np(arrays[n].dtype), kind="ExternalInput").ap() for n in _INS]
    out = nc.dram_tensor("out", (NROW, C), F32, kind="ExternalOutput").ap()
    adaln_block(nc, *args, out)
    r = run_bass_kernel_spmd(nc, [arrays], core_ids=[0])
    return r.results[0]["out"][:NTOK].reshape(NB, T, C)
```
